# Optimizing a Trainium2 kernel written in Bass

```python
import numpy as np
import jax
import jax.numpy as jnp

def _softmax(x, axis=-1):
    return jax.nn.softmax(x, axis=axis)

def _gelu(x):
    return jax.nn.gelu(x, approximate=True)

def _silu(x):
    return jax.nn.silu(x)

def _sigmoid(x):
    return jax.nn.sigmoid(x)

def _layernorm(x, axis=-1, eps=1e-05):
    m = jnp.mean(x, axis=axis, keepdims=True)
    v = jnp.var(x, axis=axis, keepdims=True)
    return (x - m) / jnp.sqrt(v + eps)

def _scatter_add(tgt, idx, src, axis=0):
    return tgt.at[idx].add(src)

def _segment_sum(src, seg, n):
    return jax.ops.segment_sum(src, seg, n)
kernel_name = 'mk_adaln_d1_jaxref_r4_e0a3e5'

def setup_inputs(seed: int=0):
    np.random.seed(seed)
    _w = jnp.asarray

    def _L0_attn_setup():
        import math
        import jax, jax.numpy as jnp
        import numpy as np
        IN_F, OUT_F, HID = (1024, 1024, 1024)
        WINDOW, STRIPES = (6, 3)

        def make_sparse_mask(n_in=IN_F, n_out=OUT_F, window=WINDOW, stripes=STRIPES):
            m = np.zeros((n_in, n_out), dtype=np.float32)
            stride = int(math.sqrt(n_in))
            for k in range(stripes):
                ps = stride * k
                for i in range(0, n_in, window):
                    m[ps + i:ps + i + window, i:i + window] = 1.0
            mb = m.astype(bool)
            return jnp.asarray((mb | mb.T).astype(np.float32))
        key = jax.random.key(seed)
        k1, k2, k3, k4 = jax.random.split(key, 4)
        scale = 1.0 / math.sqrt(IN_F)
        x = jax.random.normal(k1, (8, 192, IN_F), dtype=jnp.float32)
        w1 = jax.random.normal(k2, (HID, IN_F), dtype=jnp.float32) * scale
        w2 = jax.random.normal(k3, (OUT_F, HID), dtype=jnp.float32) * scale
        b2 = jax.random.normal(k4, (OUT_F,), dtype=jnp.float32) * scale
        return {'x': x, 'w1': w1, 'w2': w2, 'b2': b2, 'sparse_mask': make_sparse_mask()}
    _L0_attn_in = _L0_attn_setup()

    def _L0_ffn_setup():
        import jax, jax.numpy as jnp
        import numpy as np
        HIDDEN = 1024
        INTER = 2752
        RANK = 256
        B, S = (2, 512)
        key = jax.random.key(seed)
        ks = jax.random.split(key, 7)
        sc = 0.02
        return {'x': jax.random.normal(ks[0], (B, S, HIDDEN), dtype=jnp.float32), 'U1': jax.random.normal(ks[1], (HIDDEN, RANK), dtype=jnp.float32) * sc, 'V1': jax.random.normal(ks[2], (RANK, 2 * INTER), dtype=jnp.float32) * sc, 'U2': jax.random.normal(ks[3], (INTER, RANK), dtype=jnp.float32) * sc, 'V2': jax.random.normal(ks[4], (RANK, HIDDEN), dtype=jnp.float32) * sc, 'b1': jax.random.normal(ks[5], (2 * INTER,), dtype=jnp.float32) * sc, 'b2': jax.random.normal(ks[6], (HIDDEN,), dtype=jnp.float32) * sc}
    _L0_ffn_in = _L0_ffn_setup()
    _L0_c = _w((lambda *s: np.random.randn(*s).astype(np.float32) * 0.05)(8, 1024))
    _L0_wmod = _w((lambda *s: np.random.randn(*s).astype(np.float32) * 0.05)(1024, 6 * 1024) * 1024 ** (-0.5))
    _d = {'L0_attn_x': _L0_attn_in['x'], 'L0_attn_w1': _L0_attn_in['w1'], 'L0_attn_w2': _L0_attn_in['w2'], 'L0_attn_b2': _L0_attn_in['b2'], 'L0_attn_sparse_mask': _L0_attn_in['sparse_mask'], 'L0_ffn_U1': _L0_ffn_in['U1'], 'L0_ffn_V1': _L0_ffn_in['V1'], 'L0_ffn_U2': _L0_ffn_in['U2'], 'L0_ffn_V2': _L0_ffn_in['V2'], 'L0_ffn_b1': _L0_ffn_in['b1'], 'L0_ffn_b2': _L0_ffn_in['b2'], 'L0_c': _L0_c, 'L0_wmod': _L0_wmod}
    _x0 = _d['L0_attn_x']
    _d['L0_attn_x'] = jax.random.normal(jax.random.fold_in(jax.random.key(seed), 1), (8, 512, 1024), dtype=_x0.dtype)
    del _x0
    return _d

def reference(L0_attn_x, L0_attn_w1, L0_attn_w2, L0_attn_b2, L0_attn_sparse_mask, L0_ffn_U1, L0_ffn_V1, L0_ffn_U2, L0_ffn_V2, L0_ffn_b1, L0_ffn_b2, L0_c, L0_wmod):

    def _L0_attn_ref(x, w1, w2, b2, sparse_mask):
        import math
        import jax, jax.numpy as jnp
        import numpy as np
        IN_F, OUT_F, HID = (1024, 1024, 1024)
        WINDOW, STRIPES = (6, 3)

        def make_sparse_mask(n_in=IN_F, n_out=OUT_F, window=WINDOW, stripes=STRIPES):
            m = np.zeros((n_in, n_out), dtype=np.float32)
            stride = int(math.sqrt(n_in))
            for k in range(stripes):
                ps = stride * k
                for i in range(0, n_in, window):
                    m[ps + i:ps + i + window, i:i + window] = 1.0
            mb = m.astype(bool)
            return jnp.asarray((mb | mb.T).astype(np.float32))
        attn = jnp.einsum('ds,td->st', w1, w2) * sparse_mask
        y = jnp.einsum('bds,st->bdt', x, attn) + b2
        return jax.nn.gelu(y, approximate=False)

    def _L0_ffn_ref(x, U1, V1, U2, V2, b1, b2):
        import jax, jax.numpy as jnp
        import numpy as np
        HIDDEN = 1024
        INTER = 2752
        RANK = 256
        B, S = (2, 512)
        P = jnp.einsum('bsh,hr->bsr', x, U1)
        H = jnp.einsum('bsr,rf->bsf', P, V1) + b1
        gate, up = (H[..., :INTER], H[..., INTER:])
        act = jax.nn.silu(gate) * up
        Z = jnp.einsum('bsi,ir->bsr', act, U2)
        out = jnp.einsum('bsr,rh->bsh', Z, V2) + b2
        return out
    x = L0_attn_x
    mod = (_silu(L0_c) @ L0_wmod).reshape(L0_c.shape[0], 6, 1, -1)
    sa, ca, ga, sb, cb, gb = (mod[:, 0], mod[:, 1], mod[:, 2], mod[:, 3], mod[:, 4], mod[:, 5])
    ga = (2 * (ga >= 0) - 1) * jnp.maximum(jnp.abs(ga), 0.25)
    gb = (2 * (gb >= 0) - 1) * jnp.maximum(jnp.abs(gb), 0.25)
    h = _layernorm(x, axis=-1) * (1 + ca) + sa
    x = x + ga * _L0_attn_ref(h, L0_attn_w1, L0_attn_w2, L0_attn_b2, L0_attn_sparse_mask)
    h = _layernorm(x, axis=-1) * (1 + cb) + sb
    x = x + gb * _L0_ffn_ref(h, L0_ffn_U1, L0_ffn_V1, L0_ffn_U2, L0_ffn_V2, L0_ffn_b1, L0_ffn_b2)
    return x

_drawn_inputs = setup_inputs


def setup_inputs(seed=0):
    import zlib

    import numpy as np

    out = dict(_drawn_inputs(seed))
    spreads = {}
    factors = {'L0_attn_b2': 8.0,
     'L0_ffn_U1': 8.0,
     'L0_ffn_V1': 8.0,
     'L0_ffn_U2': 8.0,
     'L0_ffn_V2': 8.0,
     'L0_ffn_b1': 26.064,
     'L0_ffn_b2': 64.0}
    for name, (base, spread) in spreads.items():
        noise = np.random.default_rng([zlib.crc32(name.encode()), seed]).standard_normal(out[name].shape)
        drawn = base * np.exp(spread * noise) if base else spread * noise
        out[name] = jnp.asarray(drawn.astype(out[name].dtype))
    for name, factor in factors.items():
        out[name] = (out[name] * factor).astype(out[name].dtype)
    return out
```

```python
from contextlib import ExitStack

import concourse.bass as bass
from concourse import mybir

F32 = mybir.dt.float32
F32R = mybir.dt.float32r
I32 = mybir.dt.int32
ACT = mybir.ActivationFunctionType
ALU = mybir.AluOpType
AX = mybir.AxisListType

P = 128
EPS = 1e-5
GATE_FLOOR = 0.25


def adaln_block(nc, x, w1, w2t, b2, mask, u1, v1, u2, v2, b1_main, b1_tail, b2f, ct, wmod, out):
    NB, TOK, D = x.shape
    FB = D // P
    TT = TOK // P
    R = u1.shape[1]
    RB = R // P
    INTER = u2.shape[0]
    IB = -(-INTER // P)
    HALF = 512
    NH = D // HALF
    width = [min(P, INTER - P * i) for i in range(IB)]
    assert TOK == HALF and IB % 2 == 0 and NB % 2 == 0 and RB == 2

    def band_cols(s):
        return max(0, P * (s - 1)), min(D, P * (s + 2))

    off_band = []
    for s in range(FB):
        lo_c, hi_c = band_cols(s)
        for a, e in ((0, lo_c), (hi_c, D)):
            while a < e:
                off_band.append((s, a, min(a + HALF, e)))
                a = min(a + HALF, e)

    SCALE1, BETA1, GA, SCALE2, BETA2 = 0, FB, 2 * FB, 3 * FB, 4 * FB
    NCOL = 4 * FB + RB

    x_tiles = x.rearrange("b (n p) d -> b p n d", p=P)
    out_tiles = out.rearrange("b (n p) d -> b n p d", p=P)
    x2_dram = nc.dram_tensor("x2_dram", [NB, TOK, D], F32, kind="Internal").ap()
    x2_store = x2_dram.rearrange("b (n p) d -> b p n d", p=P)
    x2_tiles = x2_dram.rearrange("b (n p) d -> b n p d", p=P)
    pt_dram = nc.dram_tensor("pt_dram", [NB, P, 2, RB, TOK], F32, kind="Internal").ap()
    gb_dram = nc.dram_tensor("gb_dram", [NB, 1, D], F32, kind="Internal").ap()

    with ExitStack() as ctx:
        def sem(name):
            return ctx.enter_context(nc.semaphore(name))

        def buf(scope, name, shape, dt=F32):
            return scope.enter_context(nc.sbuf_tensor(name, shape, dt))

        bank = ctx.enter_context(nc.psum_tensor("bank", [P, 8, HALF], F32))

        ident = buf(ctx, "ident", [P, P])
        table = buf(ctx, "table", [P, NB, NCOL])
        b1_sb = buf(ctx, "b1_sb", [P, IB, 2])
        b2_sb = buf(ctx, "b2_sb", [P, FB])
        minus_half = buf(ctx, "minus_half", [P, TT])
        eps = buf(ctx, "eps", [P, TT])
        p01 = ctx.enter_context(ExitStack())
        attn_hi = buf(p01, "attn_hi", [P, FB, D], F32R)
        attn_lo = buf(p01, "attn_lo", [P, FB, D], F32R)
        sh = buf(p01, "sh", [P, 2, FB, NB])
        sh_hi = buf(p01, "sh_hi", [P, 2, FB, NB], F32R)
        sh_lo = buf(p01, "sh_lo", [P, 2, FB, NB], F32R)
        with ExitStack() as p0:
            w1_sb = buf(p0, "w1_sb", [P, FB, D])
            w2t_sb = buf(p0, "w2t_sb", [P, FB, D])
            mask_sb = buf(p0, "mask_sb", [P, FB, D])
            wm_sb = buf(p0, "wm_sb", [P, 2, FB, HALF])
            masked = buf(p0, "masked", [P, 2, HALF])
            off_any = buf(p0, "off_any", [P, len(off_band)])
            off_junk = buf(p0, "off_junk", [P, HALF])
            off_max = buf(p0, "off_max", [P, 1])
            dense_flag = buf(p0, "dense_flag", [P, 1])
            c_sb = buf(p0, "c_sb", [P, FB, NB])
            c_pad = buf(p0, "c_pad", [P, FB, 32])
            mod_rows = buf(p0, "mod_rows", [P, 2, P])
            gate_sign = buf(p0, "gate_sign", [P, P])
            gate_size = buf(p0, "gate_size", [P, P])
            gate_big = buf(p0, "gate_big", [P, P])
            gb_rows = buf(p0, "gb_rows", [P, 2, P])
        with ExitStack() as p1:
            xs = buf(p1, "xs", [P, TT, D])
            nrm = buf(p1, "nrm", [P, TT, D])
            xr = buf(p1, "xr", [P, TT, D])
            g = buf(p1, "g", [P, FB, TOK])
            h1_hi = buf(p1, "h1_hi", [P, FB, TOK], F32R)
            h1_lo = buf(p1, "h1_lo", [P, FB, TOK], F32R)
            h2_hi = buf(p1, "h2_hi", [P, FB, TOK], F32R)
            h2_lo = buf(p1, "h2_lo", [P, FB, TOK], F32R)
            u1_hi = buf(p1, "u1_hi", [P, FB, R], F32R)
            u1_lo = buf(p1, "u1_lo", [P, FB, R], F32R)
            pt_st = buf(p1, "pt_st", [P, 2, RB, TOK], F32R)
            bn1 = buf(p1, "bn1", [P, TT, 2, 6])
            bn2 = buf(p1, "bn2", [P, TT, 2, 6])
            mv1 = buf(p1, "mv1", [P, TT, 2])
            mv2 = buf(p1, "mv2", [P, TT, 2])
            ve1 = buf(p1, "ve1", [P, TT])
            ve2 = buf(p1, "ve2", [P, TT])
            rstd1 = buf(p1, "rstd1", [P, TT])
            rstd2 = buf(p1, "rstd2", [P, TT])
            tick = buf(p1, "tick", [P, 1])
            now1 = buf(p1, "now1", [P, FB])
            nowy = buf(p1, "nowy", [P, 2 * FB])
            now2 = buf(p1, "now2", [P, FB + RB])
        p01.close()
        p2 = ctx
        v1_hi = buf(p2, "v1_hi", [P, RB, 2 * INTER], F32R)
        v1_lo = buf(p2, "v1_lo", [P, RB, 2 * INTER], F32R)
        u2_hi = buf(p2, "u2_hi", [P, IB, R], F32R)
        u2_lo = buf(p2, "u2_lo", [P, IB, R], F32R)
        v2_hi = buf(p2, "v2_hi", [P, RB, D], F32R)
        v2_lo = buf(p2, "v2_lo", [P, RB, D], F32R)
        pt = buf(p2, "pt", [P, 2, 2, RB, TOK], F32R)
        act = buf(p2, "act", [P, 2, TOK])
        act_hi = buf(p2, "act_hi", [P, 4, TOK], F32R)
        act_lo = buf(p2, "act_lo", [P, 4, TOK], F32R)
        z_hi = buf(p2, "z_hi", [P, RB, TOK], F32R)
        z_lo = buf(p2, "z_lo", [P, RB, TOK], F32R)
        gb_bc = buf(p2, "gb_bc", [P, D])
        b2f_bc = buf(p2, "b2f_bc", [P, D])
        with ExitStack() as p2a:
            raw = buf(p2a, "raw", [P, 3, RB * HALF])
        x2t = buf(p2, "x2t", [P, 2, D])
        ffn = buf(p2, "ffn", [P, 2, HALF])

        const_in = sem("const_in")
        w_in = sem("w_in")
        mask_in = sem("mask_in")
        wm_in = [sem("wm_in0"), sem("wm_in1")]
        consts_made = sem("consts_made")
        zero_made = sem("zero_made")
        c_ready = sem("c_ready")
        dve_step = sem("dve_step")
        off_known = sem("off_known")
        flag_known = sem("flag_known")
        attn_mm = sem("attn_mm")
        masked_ready = sem("masked_ready")
        attn_hi_ready = sem("attn_hi_ready")
        attn_lo_ready = sem("attn_lo_ready")
        dn_mm = sem("dn_mm")
        dn_masked = sem("dn_masked")
        dn_hi = sem("dn_hi")
        dn_lo = sem("dn_lo")
        mod_mm = sem("mod_mm")
        mod_rows_ready = sem("mod_rows_ready")
        mod_turned = sem("mod_turned")
        mod_read = sem("mod_read")
        sh_hi_ready = sem("sh_hi_ready")
        sh_lo_ready = sem("sh_lo_ready")
        gb_ready = sem("gb_ready")
        gb_out = sem("gb_out")
        beta_mm = sem("beta_mm")
        table_ready = sem("table_ready")
        u1_in = sem("u1_in")
        u1_hi_ready = sem("u1_hi_ready")
        u1_ready = sem("u1_ready")
        xs_in = sem("xs_in")
        xr_in = [sem("xr_in0"), sem("xr_in1")]
        x2_out = sem("x2_out")
        bn_done = sem("bn_done")
        mv1_ready = sem("mv1_ready")
        mv2_ready = sem("mv2_ready")
        ve_ready = sem("ve_ready")
        rstd1_ready = sem("rstd1_ready")
        rstd2_ready = sem("rstd2_ready")
        n1_ready = sem("n1_ready")
        n2_ready = sem("n2_ready")
        turned = sem("turned")
        hi_ready = sem("hi_ready")
        lo_ready = sem("lo_ready")
        now1_ready = sem("now1_ready")
        nowy_ready = sem("nowy_ready")
        now2_ready = sem("now2_ready")
        y_done = sem("y_done")
        gelu_done = sem("gelu_done")
        g_ready = sem("g_ready")
        back_done = sem("back_done")
        x2_ready = sem("x2_ready")
        p_done = sem("p_done")
        pt_hi_ready = sem("pt_hi_ready")
        pt_lo_ready = sem("pt_lo_ready")
        pt_out = sem("pt_out")
        raw_in = [sem(f"raw_in{i}") for i in range(3)]
        w_hi_ready = sem("w_hi_ready")
        w_ready = sem("w_ready")
        pt_in = [sem("pt_in0"), sem("pt_in1")]
        gate_done = sem("gate_done")
        up_done = sem("up_done")
        silu_done = sem("silu_done")
        act_done = sem("act_done")
        act_hi_ready = sem("act_hi_ready")
        act_lo_ready = sem("act_lo_ready")
        z_step = sem("z_step")
        z_hi_ready = sem("z_hi_ready")
        z_lo_ready = sem("z_lo_ready")
        o_mm = sem("o_mm")
        ffn_sum = sem("ffn_sum")
        ffn_ready = sem("ffn_ready")
        out_ready = sem("out_ready")
        b2f_in = sem("b2f_in")
        gb_in = sem("gb_in")
        x2t_in = [sem("x2t_in0"), sem("x2t_in1")]
        out_stored = sem("out_stored")

        NCHUNK = wmod.shape[1] // HALF
        wm_view = wmod.rearrange("(k p) n -> p k n", p=P)
        SA, CA, GA_KIND, SB, CB, GB_KIND = range(6)

        def at_start(b, early=True):
            return isinstance(b, int) and b == 0 and early

        def turn1(b):
            return 0 if isinstance(b, int) and b == 0 else b * 16 - 8

        def turn2(b):
            return b * 16 + (8 if isinstance(b, int) and b == NB - 1 else 16)

        GROUPS = [(a, min(a + HALF, INTER)) for a in range(0, INTER, HALF)]
        v1_view = v1.rearrange("(k p) f -> p k f", p=P)
        v2_view = v2.rearrange("(k p) f -> p k f", p=P)
        pieces = []
        piece_of = {}
        for q, (a, e) in enumerate(GROUPS):
            for name, base in (("gate", 0), ("up", INTER)):
                n = e - a
                pieces.append([(v1_view[:, :, base + a:base + e], P, RB, n, 0,
                                v1_hi[:, :, base + a:base + e], v1_lo[:, :, base + a:base + e])])
                piece_of[name, q] = len(pieces)
            full, rest = (e - a) // P, (e - a) % P
            i0 = a // P
            parts = [(u2[a:a + full * P, :].rearrange("(i p) r -> p i r", p=P), P, full, R, 0,
                      u2_hi[:, i0:i0 + full, :], u2_lo[:, i0:i0 + full, :])]
            if rest:
                parts.append((u2[a + full * P:e, :].rearrange("(i p) r -> p i r", i=1), rest, 1, R, full * R,
                              u2_hi[0:rest, i0 + full:i0 + full + 1, :],
                              u2_lo[0:rest, i0 + full:i0 + full + 1, :]))
            pieces.append(parts)
            piece_of["u2", q] = len(pieces)
        for h in range(NH):
            pieces.append([(v2_view[:, :, h * HALF:(h + 1) * HALF], P, RB, HALF, 0,
                            v2_hi[:, :, h * HALF:(h + 1) * HALF], v2_lo[:, :, h * HALF:(h + 1) * HALF])])
        PIECES = len(pieces)

        def raw_part(slot, part):
            _, rows, blocks, n, off, _, _ = part
            return raw[0:rows, slot, off:off + blocks * n].rearrange("p (k n) -> p k n", k=blocks)

        raw_count = []
        seen = [0, 0, 0]
        for m, parts in enumerate(pieces):
            seen[m % 3] += 16 * len(parts)
            raw_count.append(seen[m % 3])

        block = ctx.enter_context(nc.Block())

        @block.sync
        def _(sp):
            sp.dma_start(c_sb[:], ct.rearrange("(k p) b -> p k b", p=P)).then_inc(const_in, 16)
            sp.dma_start(b2_sb[:], b2[:, :]).then_inc(const_in, 16)
            sp.dma_start(b1_sb[:, 0:IB - 1, :], b1_main[:, :, :]).then_inc(const_in, 16)
            sp.dma_start(b1_sb[0:width[-1], IB - 1:IB, :], b1_tail[:, :, :]).then_inc(const_in, 16)
            sp.dma_start(w1_sb[:], w1.rearrange("(k p) s -> p k s", p=P)).then_inc(w_in, 16)
            sp.dma_start(w2t_sb[:], w2t.rearrange("(k p) t -> p k t", p=P)).then_inc(w_in, 16)
            sp.dma_start(mask_sb[:], mask.rearrange("(k p) t -> p k t", p=P)).then_inc(mask_in, 16)
            for q in range(NCHUNK):
                if q >= 2:
                    sp.wait_ge(mod_mm, q - 1)
                sp.dma_start(wm_sb[:, q % 2], wm_view[:, :, q * HALF:(q + 1) * HALF]).then_inc(wm_in[q % 2], 16)
                if q == 5:
                    sp.wait_ge(mod_mm, 1)
                    sp.dma_start(xs[:], x_tiles[0]).then_inc(xs_in, 16)
                    sp.dma_start(xr[:, 0:2, :].rearrange("p n d -> p (n d)").rearrange("p (k r) -> p k r", k=FB),
                                 u1.rearrange("(k p) r -> p k r", p=P)).then_inc(u1_in, 16)
            for half in range(2):
                sp.wait_ge(gb_ready, half + 1)
                for j in range(4):
                    c0 = half * HALF + j * P
                    sp.dma_start(gb_dram[:, 0, c0:c0 + P], gb_rows[32 * j:32 * j + NB, half, :]).then_inc(gb_out, 16)

            def iteration(b, has_y, has_prev, has_load):
                if has_y:
                    if has_prev:
                        sp.wait_ge(x2_out, b * 32)
                    else:
                        sp.wait_ge(u1_ready, 1)
                    for half in range(2):
                        n = slice(half * TT // 2, (half + 1) * TT // 2)
                        sp.dma_start(xr[:, n, :], x_tiles[b, :, n, :]).then_inc(xr_in[half], 16)
                if has_load:
                    sp.wait_ge(n1_ready, b * 4 + 8)
                    sp.dma_start(xs[:], x_tiles[b + 2]).then_inc(xs_in, 16)
                if has_y:
                    sp.wait_ge(x2_ready, b * 8 + 4)
                    sp.dma_start(x2_store[b, :, 0:TT // 2, :], xr[:, 0:TT // 2, :]).then_inc(x2_out, 16)
                if has_prev:
                    sp.wait_ge(pt_lo_ready, b * 2)
                    sp.dma_start(pt_dram[b - 1], pt_st[:].bitcast(F32)).then_inc(pt_out, 16)
                if has_y:
                    sp.wait_ge(n2_ready, b * 4 + 4)
                    sp.dma_start(x2_store[b, :, TT // 2:TT, :], xr[:, TT // 2:TT, :]).then_inc(x2_out, 16)

            sp.wait_ge(n1_ready, 4)
            sp.dma_start(xs[:], x_tiles[1]).then_inc(xs_in, 16)
            iteration(0, True, False, True)
            with sp.Fori(1, NB - 2) as b:
                iteration(b, True, True, True)
            iteration(NB - 2, True, True, False)
            iteration(NB - 1, True, True, False)
            iteration(NB, False, True, False)

            sp.wait_ge(pt_out, 16 * NB)
            sp.wait_ge(x2_out, 32 * NB)
            sp.wait_ge(gb_out, 16 * 8)
            sp.dma_start(pt[:, 0].bitcast(F32), pt_dram[0]).then_inc(pt_in[0], 16)
            for m, parts in enumerate(pieces):
                if m >= 3:
                    sp.wait_ge(w_ready, m - 2)
                for part in parts:
                    sp.dma_start(raw_part(m % 3, part), part[0]).then_inc(raw_in[m % 3], 16)
            sp.dma_start(b2f_bc[:], b2f[:, :].broadcast_to([P, D])).then_inc(b2f_in, 16)
            sp.wait_ge(w_ready, PIECES)

            def tile_in(b, n):
                sp.dma_start(x2t[:, n % 2, :], x2_tiles[b, n]).then_inc(x2t_in[n % 2], 16)

            def batch(b, q, last):
                if not last:
                    if not at_start(b):
                        sp.wait_ge(up_done, b * IB)
                    sp.dma_start(pt[:, 1 - q].bitcast(F32), pt_dram[b + 1]).then_inc(pt_in[1 - q], 16)
                if not at_start(b):
                    sp.wait_ge(ffn_ready, b * 8)
                sp.dma_start(gb_bc[:], gb_dram[b].broadcast_to([P, D])).then_inc(gb_in, 16)
                for n in range(TT):
                    sp.wait_ge(out_ready, b * 8 + 2 * n + 2)
                    sp.dma_start(out_tiles[b, n], x2t[:, n % 2, :]).then_inc(out_stored, 16)
                    sp.wait_ge(out_stored, b * 64 + 16 * n + 16)
                    if n < 2:
                        tile_in(b, n + 2)
                    elif not last:
                        tile_in(b + 1, n - 2)

            tile_in(0, 0)
            tile_in(0, 1)
            batch(0, 0, False)
            with sp.Fori(1, NB // 2) as i:
                batch(i * 2 - 1, 1, False)
                batch(i * 2, 0, False)
            batch(NB - 1, 1, True)
            sp.wait_ge(out_stored, 64 * NB)

        @block.tensor
        def _(pe):
            def three(acc, s_hi, s_lo, m_hi, m_lo, start, stop):
                nc.tensor.matmul(acc, s_hi, m_hi, start=start, stop=False)
                nc.tensor.matmul(acc, s_hi, m_lo, start=False, stop=False)
                return nc.tensor.matmul(acc, s_lo, m_hi, start=False, stop=stop)

            def attn_product(acc, s, a, e):
                for k in range(FB):
                    last = nc.tensor.matmul(acc, w1_sb[:, k, s * P:(s + 1) * P], w2t_sb[:, k, a:e],
                                            start=(k == 0), stop=(k == FB - 1))
                return last

            pe.wait_ge(w_in, 32)
            for s in range(FB):
                a, e = band_cols(s)
                if s >= 2:
                    pe.wait_ge(masked_ready, s - 1)
                attn_product(bank[:, s % 2, 0:e - a], s, a, e).then_inc(attn_mm, 1)
            pe.wait_ge(flag_known, 1)
            dense = nc.tensor.value_load(dense_flag[0:1, 0:1].bitcast(I32))
            with nc.tensor.If(dense != 0):
                pe.wait_ge(masked_ready, FB)
                for n, (s, a, e) in enumerate(off_band):
                    if n >= 2:
                        pe.wait_ge(dn_masked, n - 1)
                    attn_product(bank[:, n % 2, 0:e - a], s, a, e).then_inc(dn_mm, 1)

            def mod_product(q):
                pe.wait_ge(wm_in[q % 2], 16 * (q // 2 + 1))
                if q >= 2:
                    pe.wait_ge(mod_rows_ready, q - 1)
                for k in range(FB):
                    for j in range(4):
                        last = nc.tensor.matmul(bank[32 * j:32 * j + 32, 2 + q % 2, 0:P], c_pad[:, k, :],
                                                wm_sb[:, q % 2, k, j * P:(j + 1) * P],
                                                start=(k == 0), stop=(k == FB - 1), skip_group_check=True)
                last.then_inc(mod_mm, 1)

            def mod_turn(q):
                pe.wait_ge(mod_rows_ready, q + 1)
                if q >= 2:
                    pe.wait_ge(mod_read, q - 1)
                nc.tensor.transpose(bank[:, 4 + q % 2, 0:P], mod_rows[:, q % 2, :], ident[:]).then_inc(mod_turned, 1)

            pe.wait_ge(consts_made, 1)
            pe.wait_ge(c_ready, 1)
            for q in range(NCHUNK):
                mod_product(q)
                if 1 <= q <= NCHUNK - 2:
                    mod_turn(q - 1)
            pe.wait_ge(sh_lo_ready, 1)
            pe.wait_ge(attn_lo_ready, FB)
            for t in range(FB):
                near = [s for s in range(FB) if abs(s - t) <= 1]
                acc = bank[:, 6, t * NB:(t + 1) * NB]
                cols = slice(t * P, (t + 1) * P)
                for s in near:
                    last = three(acc, attn_hi[:, s, cols], attn_lo[:, s, cols], sh_hi[:, 0, s, :], sh_lo[:, 0, s, :],
                                 s == near[0], s == near[-1])
            last.then_inc(beta_mm, 1)
            with nc.tensor.If(dense != 0):
                pe.wait_ge(dn_lo, len(off_band))
                for t in range(FB):
                    far = [s for s in range(FB) if abs(s - t) > 1]
                    acc = bank[:, 7, t * NB:(t + 1) * NB]
                    cols = slice(t * P, (t + 1) * P)
                    for s in far:
                        last = three(acc, attn_hi[:, s, cols], attn_lo[:, s, cols], sh_hi[:, 0, s, :],
                                     sh_lo[:, 0, s, :], s == far[0], s == far[-1])
                last.then_inc(dn_mm, 1)

            def y(b, t):
                first = turn1(b)
                if not at_start(b, t < 2):
                    pe.wait_ge(gelu_done, b * 8 + t - 1)
                pe.wait_ge(lo_ready, first + min(t + 2, FB))
                near = [s for s in range(FB) if abs(s - t) <= 1]
                far = [s for s in range(FB) if abs(s - t) > 1]
                acc = bank[:, t % 2, :]
                cols = slice(t * P, (t + 1) * P)
                for s in near[:-1]:
                    three(acc, attn_hi[:, s, cols], attn_lo[:, s, cols], h1_hi[:, s, :], h1_lo[:, s, :],
                          s == near[0], False)
                with nc.tensor.If(dense != 0):
                    pe.wait_ge(lo_ready, first + FB)
                    for s in far:
                        three(acc, attn_hi[:, s, cols], attn_lo[:, s, cols], h1_hi[:, s, :], h1_lo[:, s, :],
                              False, False)
                s = near[-1]
                three(acc, attn_hi[:, s, cols], attn_lo[:, s, cols], h1_hi[:, s, :], h1_lo[:, s, :],
                      False, True).then_inc(y_done, 1)

            def turn(number, k):
                if not (isinstance(number, int) and number < 2):
                    pe.wait_ge(lo_ready, number - 1)
                for n in range(TT):
                    last = nc.tensor.transpose(bank[:, 2 + k % 2, n * P:(n + 1) * P],
                                               nrm[:, n, k * P:(k + 1) * P], ident[:])
                last.then_inc(turned, 1)

            def turn_back(b, k):
                if not at_start(b, k < 2):
                    pe.wait_ge(x2_ready, b * 8 + k - 1)
                if k == 0:
                    pe.wait_ge(g_ready, b * 8 + 8)
                n = k // 2
                for j in range(4):
                    last = nc.tensor.transpose(bank[:, 4 + k % 2, j * P:(j + 1) * P],
                                               g[:, 4 * (k % 2) + j, n * P:(n + 1) * P], ident[:])
                last.then_inc(back_done, 1)

            def p_product(b, k):
                pe.wait_ge(lo_ready, turn2(b) + k + 1)
                if k == 0 and not at_start(b):
                    pe.wait_ge(pt_lo_ready, b * 2)
                for r in range(RB):
                    cols = slice(r * P, (r + 1) * P)
                    last = three(bank[:, 6 + r, :], u1_hi[:, k, cols], u1_lo[:, k, cols],
                                 h2_hi[:, k, :], h2_lo[:, k, :], k == 0, k == FB - 1)
                if k == FB - 1:
                    last.then_inc(p_done, 1)

            def iteration(b, has_y, has_prev, has_next):
                for t in range(FB):
                    if has_y:
                        y(b, t)
                    if has_prev and 3 <= t <= 6:
                        if t == 3:
                            pe.wait_ge(n2_ready, b * 4)
                        for k in (2 * (t - 3), 2 * (t - 3) + 1):
                            turn(turn2(b - 1) + k, k)
                for k in range(FB):
                    if has_prev:
                        p_product(b - 1, k)
                    if has_y:
                        turn_back(b, k)
                    if has_next:
                        if k == 0:
                            pe.wait_ge(n1_ready, b * 4 + 8)
                        turn(turn1(b + 1) + k, k)

            pe.wait_ge(n1_ready, 4)
            pe.wait_ge(mod_rows_ready, NCHUNK)
            for k in range(FB):
                turn(k, k)
            iteration(0, True, False, True)
            pe.wait_ge(table_ready, 1)
            pe.wait_ge(sh_lo_ready, 2)
            pe.wait_ge(u1_ready, 1)
            for r in range(RB):
                acc = bank[:, 6, r * NB:(r + 1) * NB]
                cols = slice(r * P, (r + 1) * P)
                for k in range(FB):
                    last = three(acc, u1_hi[:, k, cols], u1_lo[:, k, cols], sh_hi[:, 1, k, :], sh_lo[:, 1, k, :],
                                 k == 0, k == FB - 1)
            last.then_inc(beta_mm, 1)
            pe.wait_ge(table_ready, 2)
            with pe.Fori(1, NB - 1) as b:
                iteration(b, True, True, True)
            iteration(NB - 1, True, True, False)
            iteration(NB, False, True, False)

            def h_product(b, q, i):
                if i == 0:
                    pe.wait_ge(pt_in[q], (b - q) * 8 + 16)
                if not at_start(b, i < 2):
                    pe.wait_ge(act_done, b * IB + i - 1)
                w = width[i]
                for name, first_bank, base, done in (("gate", 0, 0, gate_done), ("up", 2, INTER, up_done)):
                    if i % 4 == 0:
                        pe.wait_ge(w_ready, piece_of[name, i // 4])
                    cols = slice(base + i * P, base + i * P + w)
                    for r in range(RB):
                        last = three(bank[0:w, first_bank + i % 2, :], v1_hi[:, r, cols], v1_lo[:, r, cols],
                                     pt[:, q, 0, r, :], pt[:, q, 1, r, :], r == 0, r == RB - 1)
                    last.then_inc(done, 1)

            def z_product(b, q, i):
                pe.wait_ge(act_lo_ready, b * IB + i + 1)
                if i % 4 == 0:
                    pe.wait_ge(w_ready, piece_of["u2", i // 4])
                if i == 0 and not at_start(b):
                    pe.wait_ge(z_lo_ready, b * 2)
                w = width[i]
                slot = (q * IB + i) % 4
                for r in range(RB):
                    cols = slice(r * P, (r + 1) * P)
                    last = three(bank[:, 4 + r, :], u2_hi[0:w, i, cols], u2_lo[0:w, i, cols],
                                 act_hi[0:w, slot, :], act_lo[0:w, slot, :], i == 0, i == IB - 1)
                last.then_inc(z_step, 1)

            def out_product(b):
                pe.wait_ge(z_lo_ready, b * 2 + 2)
                pe.wait_ge(w_ready, PIECES)
                for m in range(TT * NH):
                    n, h = m // NH, m % NH
                    if not at_start(b, m < 2):
                        pe.wait_ge(ffn_sum, b * 8 + max(m - 1, 0))
                    toks, cols = slice(n * P, (n + 1) * P), slice(h * HALF, (h + 1) * HALF)
                    for r in range(RB):
                        last = three(bank[:, 6 + m % 2, :], z_hi[:, r, toks], z_lo[:, r, toks],
                                     v2_hi[:, r, cols], v2_lo[:, r, cols], r == 0, r == RB - 1)
                    last.then_inc(o_mm, 1)

            def batch(b, q, last):
                for i in range(2, IB):
                    h_product(b, q, i)
                    z_product(b, q, i - 2)
                if not last:
                    h_product(b + 1, 1 - q, 0)
                z_product(b, q, IB - 2)
                z_product(b, q, IB - 1)
                if not last:
                    h_product(b + 1, 1 - q, 1)
                out_product(b)

            pe.wait_ge(gelu_done, 8 * NB)
            pe.wait_ge(x2_ready, 8 * NB)
            pe.wait_ge(lo_ready, turn2(NB - 1) + FB)
            pe.wait_ge(pt_lo_ready, 2 * NB)
            h_product(0, 0, 0)
            h_product(0, 0, 1)
            batch(0, 0, False)
            with pe.Fori(1, NB // 2) as i:
                batch(i * 2 - 1, 1, False)
                batch(i * 2, 0, False)
            batch(NB - 1, 1, True)

        @block.scalar
        def _(ae):
            ae.wait_ge(const_in, 64)
            ae.wait_ge(zero_made, 1)
            nc.scalar.activation(c_pad[:, :, 0:NB], c_sb[:], ACT.Silu).then_inc(c_ready, 1)
            for s in range(FB):
                a, e = band_cols(s)
                ae.wait_ge(masked_ready, s + 1)
                nc.scalar.activation(attn_hi[:, s, a:e], masked[:, s % 2, 0:e - a], ACT.Copy).then_inc(attn_hi_ready, 1)
            ae.wait_ge(flag_known, 1)
            dense = nc.scalar.value_load(dense_flag[0:1, 0:1].bitcast(I32))
            with nc.scalar.If(dense != 0):
                for n, (s, a, e) in enumerate(off_band):
                    ae.wait_ge(dn_masked, n + 1)
                    nc.scalar.activation(attn_hi[:, s, a:e], masked[:, n % 2, 0:e - a], ACT.Copy).then_inc(dn_hi, 1)
            for v in range(2):
                ae.wait_ge(mod_read, (2, 8)[v])
                nc.scalar.activation(sh_hi[:, v], sh[:, v], ACT.Copy).then_inc(sh_hi_ready, 1)

            def hi(number, k, h_hi, scale):
                ae.wait_ge(turned, number + k + 1)
                nc.scalar.activation(h_hi[:, k, :], bank[:, 2 + k % 2, :], ACT.Copy,
                                     scale=scale[:, k:k + 1]).then_inc(hi_ready, 1)

            def gelu(b, t):
                ae.wait_ge(y_done, b * 8 + t + 1)
                nc.scalar.activation(g[:, t, :], bank[:, t % 2, :], ACT.Gelu,
                                     bias=nowy[:, t:t + 1]).then_inc(gelu_done, 1)

            def load_now1(b):
                if not at_start(b):
                    ae.wait_ge(lo_ready, turn1(b - 1) + FB)
                    ae.wait_ge(y_done, b * 8)
                nc.scalar.activation(now1[:], table[:, b, SCALE1:SCALE1 + FB], ACT.Copy).then_inc(now1_ready, 1)
                ae.wait_ge(now1_ready, b + 1)

            def iteration(b, has_y, has_prev, has_next):
                if has_y:
                    if not has_prev:
                        ae.wait_ge(table_ready, 1)
                    else:
                        ae.wait_ge(back_done, b * 8)
                    nc.scalar.activation(nowy[:], table[:, b, BETA1:BETA1 + 2 * FB],
                                         ACT.Copy).then_inc(nowy_ready, 1)
                    ae.wait_ge(nowy_ready, b + 1)
                if has_prev:
                    ae.wait_ge(table_ready, 2)
                    if not at_start(b - 1):
                        ae.wait_ge(pt_lo_ready, b * 2 - 2)
                    nc.scalar.activation(now2[:], table[:, b - 1, SCALE2:SCALE2 + FB + RB],
                                         ACT.Copy).then_inc(now2_ready, 1)
                    ae.wait_ge(now2_ready, b)
                for t in range(FB):
                    if has_y:
                        gelu(b, t)
                    if has_prev and 3 <= t <= 6:
                        for k in (2 * (t - 3), 2 * (t - 3) + 1):
                            hi(turn2(b - 1), k, h2_hi, now2)
                if has_next:
                    load_now1(b + 1)
                    for k in range(FB):
                        hi(turn1(b + 1), k, h1_hi, now1)
                if has_prev:
                    ae.wait_ge(p_done, b)
                    if not at_start(b - 1):
                        ae.wait_ge(pt_out, b * 16 - 16)
                    for r in range(RB):
                        nc.scalar.activation(pt_st[:, 0, r, :], bank[:, 6 + r, :], ACT.Identity,
                                             bias=now2[:, FB + r:FB + r + 1]).then_inc(pt_hi_ready, 1)

            ae.wait_ge(mod_read, 4)
            load_now1(0)
            for k in range(FB):
                hi(0, k, h1_hi, now1)
            iteration(0, True, False, True)
            iteration(1, True, True, True)
            with ae.Fori(2, NB - 1) as b:
                iteration(b, True, True, True)
            iteration(NB - 1, True, True, False)
            iteration(NB, False, True, False)

            def silu(b, q, i):
                w = width[i]
                ae.wait_ge(gate_done, b * IB + i + 1)
                if not at_start(b, i < 2):
                    ae.wait_ge(act_lo_ready, b * IB + i - 1)
                nc.scalar.activation(act[0:w, i % 2, :], bank[0:w, i % 2, :], ACT.Silu,
                                     bias=b1_sb[0:w, i, 0:1]).then_inc(silu_done, 1)

            def act_hi_part(b, q, i):
                w = width[i]
                slot = (q * IB + i) % 4
                ae.wait_ge(act_done, b * IB + i + 1)
                if not at_start(b, i < 4):
                    ae.wait_ge(z_step, b * IB + max(i - 3, 0))
                nc.scalar.activation(act_hi[0:w, slot, :], act[0:w, i % 2, :], ACT.Copy).then_inc(act_hi_ready, 1)

            def batch(b, q, last):
                for i in range(1, IB):
                    silu(b, q, i)
                    act_hi_part(b, q, i - 1)
                if not last:
                    silu(b + 1, 1 - q, 0)
                act_hi_part(b, q, IB - 1)
                ae.wait_ge(z_step, b * IB + IB)
                if not at_start(b):
                    ae.wait_ge(o_mm, b * 8)
                for r in range(RB):
                    nc.scalar.activation(z_hi[:, r, :], bank[:, 4 + r, :], ACT.Copy).then_inc(z_hi_ready, 1)

            silu(0, 0, 0)
            batch(0, 0, False)
            with ae.Fori(1, NB // 2) as i:
                batch(i * 2 - 1, 1, False)
                batch(i * 2, 0, False)
            batch(NB - 1, 1, True)

        @block.vector
        def _(dve):
            steps = [0]

            def link(ins):
                steps[0] += 1
                ins.then_inc(dve_step, 1)
                dve.wait_ge(dve_step, steps[0])

            dve.wait_ge(mask_in, 16)
            for n, (s, a, e) in enumerate(off_band):
                link(nc.vector.tensor_scalar(off_junk[:, 0:e - a], mask_sb[:, s, a:e], 0.0, 0.0, ALU.not_equal,
                                             ALU.max, accum_out=off_any[:, n:n + 1]))
            nc.vector.tensor_reduce(off_max[:], off_any[:], AX.X, ALU.max).then_inc(off_known, 1)

            def mask_product(src_bank, slot, s, a, e, ready):
                nc.vector.tensor_tensor(masked[:, slot, 0:e - a], bank[:, src_bank, 0:e - a], mask_sb[:, s, a:e],
                                        ALU.mult).then_inc(ready, 1)

            def attn_rest(slot, s, a, e, ready):
                nc.vector.tensor_tensor(attn_lo[:, s, a:e], masked[:, slot, 0:e - a], attn_hi[:, s, a:e],
                                        ALU.subtract).then_inc(ready, 1)

            for s in range(FB):
                a, e = band_cols(s)
                dve.wait_ge(attn_mm, s + 1)
                if s >= 2:
                    dve.wait_ge(attn_lo_ready, s - 1)
                mask_product(s % 2, s % 2, s, a, e, masked_ready)
                dve.wait_ge(attn_hi_ready, s + 1)
                attn_rest(s % 2, s, a, e, attn_lo_ready)
            dve.wait_ge(flag_known, 1)
            dense = nc.vector.value_load(dense_flag[0:1, 0:1].bitcast(I32))
            with nc.vector.If(dense != 0):
                dve.wait_ge(attn_lo_ready, FB)
                for n, (s, a, e) in enumerate(off_band):
                    dve.wait_ge(dn_mm, n + 1)
                    if n >= 2:
                        dve.wait_ge(dn_lo, n - 1)
                    mask_product(n % 2, n % 2, s, a, e, dn_masked)
                    dve.wait_ge(dn_hi, n + 1)
                    attn_rest(n % 2, s, a, e, dn_lo)

            def clamp_gate(dst, src, sign, size, big, count):
                nc.vector.tensor_scalar(sign, src, 0.0, 2.0, ALU.is_ge, ALU.mult)
                link(nc.vector.scalar_tensor_tensor(size, src, -1.0, src, ALU.mult, ALU.max))
                link(nc.vector.tensor_scalar(big, size, GATE_FLOOR, None, ALU.max))
                return nc.vector.scalar_tensor_tensor(dst, sign, -1.0, big, ALU.add, ALU.mult)

            def mod_copy(q):
                dve.wait_ge(mod_mm, q + 1)
                if 2 <= q:
                    dve.wait_ge(mod_turned, min(q - 1, NCHUNK - 2))
                nc.vector.tensor_copy(mod_rows[:, q % 2, :], bank[:, 2 + q % 2, 0:P]).then_inc(mod_rows_ready, 1)

            def mod_place(q):
                kind, half = q // 2, q % 2
                dve.wait_ge(mod_turned, q + 1)
                src = bank[:, 4 + q % 2, 0:P].rearrange("p (j c) -> p j c", j=4)[:, :, 0:NB]
                j0 = half * 4
                if kind in (SA, SB):
                    nc.vector.tensor_copy(sh[:, kind // 3, j0:j0 + 4, :], src).then_inc(mod_read, 1)
                else:
                    base = {CA: SCALE1, GA_KIND: GA, CB: SCALE2}[kind] + j0
                    dst = table[:, :, base:base + 4].rearrange("p b j -> p j b")
                    add = 0.0 if kind == GA_KIND else 1.0
                    nc.vector.tensor_scalar(dst, src, add, None, ALU.add).then_inc(mod_read, 1)

            def stats1(b, tiles):
                dve.wait_ge(xs_in, b * 16 + 16)
                for n in tiles:
                    for h in range(NH):
                        nc.vector.bn_stats(bn1[:, n, h, :], xs[:, n, h * HALF:(h + 1) * HALF]).then_inc(bn_done, 1)

            def aggregate(bn, mv, n, count, ready):
                if count is not None:
                    dve.wait_ge(bn_done, count)
                    nc.vector.memset(tick[:], 0.0)
                nc.vector.bn_aggr(mv[:, n, :], bn[:, n, :, :].rearrange("p h s -> p (h s)")).then_inc(ready, 1)

            def normalise(src, mv, rstd, ready):
                for n in range(TT):
                    nc.vector.tensor_scalar(nrm[:, n, :], src[:, n, :], mv[:, n, 0:1], rstd[:, n:n + 1],
                                            ALU.subtract, ALU.mult).then_inc(ready, 1)

            for q in range(NCHUNK):
                if q == NCHUNK - 3:
                    stats1(0, range(TT))
                    for n in range(TT):
                        aggregate(bn1, mv1, n, 8 if n == 0 else None, mv1_ready)
                    dve.wait_ge(rstd1_ready, 1)
                    normalise(xs, mv1, rstd1, n1_ready)
                mod_copy(q)
                if 1 <= q <= NCHUNK - 2:
                    mod_place(q - 1)
                if q >= NCHUNK - 2:
                    dve.wait_ge(mod_rows_ready, q + 1)
                    clamp_gate(gb_rows[:, q % 2, :], mod_rows[:, q % 2, :], gate_sign[:], gate_size[:], gate_big[:],
                               None).then_inc(gb_ready, 1)
                    dve.wait_ge(gb_ready, q - NCHUNK + 3)
            ga_cols = table[:, :, GA:GA + FB]
            shape3 = lambda m: m[:, 0:NB * FB].rearrange("p (b f) -> p b f", b=NB)
            dve.wait_ge(mod_read, 6)
            link(clamp_gate(ga_cols, ga_cols, shape3(gate_sign), shape3(gate_size), shape3(gate_big), None))
            for v in range(2):
                dve.wait_ge(sh_hi_ready, v + 1)
                nc.vector.tensor_tensor(sh_lo[:, v], sh[:, v], sh_hi[:, v], ALU.subtract).then_inc(sh_lo_ready, 1)
            dve.wait_ge(beta_mm, 1)
            for t in range(FB):
                nc.vector.tensor_scalar(table[:, :, BETA1 + t], bank[:, 6, t * NB:(t + 1) * NB], b2_sb[:, t:t + 1],
                                        None, ALU.add).then_inc(dve_step, 1)
            steps[0] += FB
            dve.wait_ge(dve_step, steps[0])
            with nc.vector.If(dense != 0):
                dve.wait_ge(dn_mm, len(off_band) + 1)
                for t in range(FB):
                    nc.vector.tensor_tensor(table[:, :, BETA1 + t], bank[:, 7, t * NB:(t + 1) * NB],
                                            table[:, :, BETA1 + t], ALU.add).then_inc(dn_lo, 1)
                dve.wait_ge(dn_lo, len(off_band) + FB)
            nc.vector.tensor_scalar(minus_half[:], minus_half[:], 1.0, None, ALU.mult).then_inc(table_ready, 1)

            def lo(number, k, h_hi, h_lo, scale):
                dve.wait_ge(hi_ready, number + k + 1)
                nc.vector.scalar_tensor_tensor(h_lo[:, k, :], bank[:, 2 + k % 2, :], scale[:, k:k + 1],
                                               h_hi[:, k, :], ALU.mult, ALU.subtract).then_inc(lo_ready, 1)

            def iteration(b, has_y, has_prev, has_next):
                if has_prev:
                    dve.wait_ge(rstd2_ready, b)
                    dve.wait_ge(turned, turn2(NB - 1) if isinstance(b, int) and b == NB else turn1(b) + FB)
                    normalise(xr, mv2, rstd2, n2_ready)
                if has_next:
                    stats1(b + 1, (0, 1))
                if has_prev:
                    for k in range(0, 4):
                        lo(turn2(b - 1), k, h2_hi, h2_lo, now2)
                if has_next:
                    stats1(b + 1, (2, 3))
                    for n in range(TT):
                        aggregate(bn1, mv1, n, b * 16 + 16 if n == 0 else None, mv1_ready)
                if has_prev:
                    for k in range(4, FB):
                        lo(turn2(b - 1), k, h2_hi, h2_lo, now2)
                if has_next:
                    dve.wait_ge(rstd1_ready, b + 2)
                    dve.wait_ge(turned, turn2(b - 1) + FB if has_prev else FB)
                    normalise(xs, mv1, rstd1, n1_ready)
                for k in range(FB):
                    n, h = k // NH, k % NH
                    if has_y:
                        dve.wait_ge(back_done, b * 8 + k + 1)
                        if k % 4 == 0:
                            dve.wait_ge(xr_in[k // 4], b * 16 + 16)
                        half = xr[:, n, h * HALF:(h + 1) * HALF]
                        nc.vector.tensor_tensor(half, bank[:, 4 + h, :], half, ALU.add).then_inc(x2_ready, 1)
                    if has_next:
                        lo(turn1(b + 1), k, h1_hi, h1_lo, now1)
                    if has_y:
                        dve.wait_ge(x2_ready, b * 8 + k + 1)
                        nc.vector.bn_stats(bn2[:, n, h, :], half).then_inc(bn_done, 1)
                        if h == 1:
                            after = b * 16 + 16 if has_next else b * 16 + 8
                            aggregate(bn2, mv2, n, after + k + 1, mv2_ready)
                if has_prev:
                    for r in range(RB):
                        dve.wait_ge(pt_hi_ready, b * 2 - 1 + r)
                        nc.vector.scalar_tensor_tensor(pt_st[:, 1, r, :], bank[:, 6 + r, :],
                                                       now2[:, FB + r:FB + r + 1], pt_st[:, 0, r, :],
                                                       ALU.add, ALU.subtract).then_inc(pt_lo_ready, 1)

            for k in range(FB):
                lo(0, k, h1_hi, h1_lo, now1)
            iteration(0, True, False, True)
            dve.wait_ge(beta_mm, 2)
            for r in range(RB):
                last = nc.vector.tensor_copy(table[:, :, BETA2 + r], bank[:, 6, r * NB:(r + 1) * NB])
            last.then_inc(table_ready, 1)
            with dve.Fori(1, NB - 1) as b:
                iteration(b, True, True, True)
            iteration(NB - 1, True, True, False)
            iteration(NB, False, True, False)

            def multiply(b, q, i):
                w = width[i]
                dve.wait_ge(up_done, b * IB + i + 1)
                dve.wait_ge(silu_done, b * IB + i + 1)
                nc.vector.scalar_tensor_tensor(act[0:w, i % 2, :], bank[0:w, 2 + i % 2, :], b1_sb[0:w, i, 1:2],
                                               act[0:w, i % 2, :], ALU.add, ALU.mult).then_inc(act_done, 1)

            def act_lo_part(b, q, i):
                w = width[i]
                slot = (q * IB + i) % 4
                dve.wait_ge(act_hi_ready, b * IB + i + 1)
                nc.vector.tensor_tensor(act_lo[0:w, slot, :], act[0:w, i % 2, :], act_hi[0:w, slot, :],
                                        ALU.subtract).then_inc(act_lo_ready, 1)

            def batch(b, q, last):
                for i in range(1, IB):
                    multiply(b, q, i)
                    act_lo_part(b, q, i - 1)
                if not last:
                    multiply(b + 1, 1 - q, 0)
                act_lo_part(b, q, IB - 1)
                for r in range(RB):
                    dve.wait_ge(z_hi_ready, b * 2 + r + 1)
                    nc.vector.tensor_tensor(z_lo[:, r, :], bank[:, 4 + r, :], z_hi[:, r, :],
                                            ALU.subtract).then_inc(z_lo_ready, 1)
                if isinstance(b, int) and b == 0:
                    dve.wait_ge(b2f_in, 16)
                for m in range(TT * NH):
                    cols = slice((m % NH) * HALF, (m % NH + 1) * HALF)
                    dve.wait_ge(o_mm, b * 8 + m + 1)
                    if not at_start(b, m < 2):
                        dve.wait_ge(out_ready, b * 8 + max(m - 1, 0))
                    nc.vector.tensor_tensor(ffn[:, m % 2, :], bank[:, 6 + m % 2, :], b2f_bc[:, cols],
                                            ALU.add).then_inc(ffn_sum, 1)
                    if m == 0:
                        dve.wait_ge(gb_in, b * 16 + 16)
                    dve.wait_ge(ffn_sum, b * 8 + m + 1)
                    nc.vector.tensor_tensor(ffn[:, m % 2, :], ffn[:, m % 2, :], gb_bc[:, cols],
                                            ALU.mult).then_inc(ffn_ready, 1)

            multiply(0, 0, 0)
            batch(0, 0, False)
            with dve.Fori(1, NB // 2) as i:
                batch(i * 2 - 1, 1, False)
                batch(i * 2, 0, False)
            batch(NB - 1, 1, True)

        @block.gpsimd
        def _(pool):
            nc.gpsimd.memset(c_pad[:], 0.0).then_inc(zero_made, 1)
            nc.gpsimd.memset(ident[:], 0.0).then_inc(zero_made, 1)
            nc.gpsimd.memset(minus_half[:], -0.5).then_inc(zero_made, 1)
            nc.gpsimd.memset(eps[:], EPS).then_inc(zero_made, 1)
            pool.wait_ge(zero_made, 4)
            nc.gpsimd.affine_select(out=ident[:], in_=ident[:], compare_op=ALU.not_equal, fill=1.0, base=0,
                                    pattern=[[-1, P]], channel_multiplier=1).then_inc(consts_made, 1)
            pool.wait_ge(off_known, 1)
            nc.gpsimd.partition_all_reduce(dense_flag[:], off_max[:], P, bass.bass_isa.ReduceOp.max)\
                .then_inc(flag_known, 1)

            def rstd(mv, ve, dst, mv_ready, count, ve_count, ready):
                pool.wait_ge(mv_ready, count)
                nc.gpsimd.tensor_tensor(ve[:], mv[:, :, 1], eps[:], ALU.add).then_inc(ve_ready, 1)
                pool.wait_ge(ve_ready, ve_count)
                nc.gpsimd.tensor_tensor(dst[:], ve[:], minus_half[:], ALU.pow).then_inc(ready, 1)

            def gate(b, t):
                pool.wait_ge(gelu_done, b * 8 + t + 1)
                nc.gpsimd.tensor_tensor(g[:, t, :], g[:, t, :], nowy[:, FB + t:FB + t + 1].to_broadcast([P, TOK]),
                                        ALU.mult).then_inc(g_ready, 1)

            rstd(mv1, ve1, rstd1, mv1_ready, 4, 1, rstd1_ready)
            pool.wait_ge(u1_in, 16)
            pool.wait_ge(mod_mm, NCHUNK)
            pool.wait_ge(gb_out, 16 * 8)
            pool.wait_ge(sh_lo_ready, 2)
            u1_raw = xr[:, 0:2, :].rearrange("p n d -> p (n d)").rearrange("p (k r) -> p k r", k=FB)
            nc.gpsimd.tensor_copy(u1_hi[:], u1_raw).then_inc(u1_hi_ready, 1)
            pool.wait_ge(u1_hi_ready, 1)
            nc.gpsimd.tensor_tensor(u1_lo[:], u1_raw, u1_hi[:], ALU.subtract).then_inc(u1_ready, 1)

            def iteration(b, has_next):
                for t in range(5):
                    gate(b, t)
                if has_next:
                    rstd(mv1, ve1, rstd1, mv1_ready, b * 4 + 8, b * 2 + 2, rstd1_ready)
                for t in range(5, FB):
                    gate(b, t)
                rstd(mv2, ve2, rstd2, mv2_ready, b * 4 + 4, b * 2 + 3 if has_next else b * 2 + 2, rstd2_ready)

            with pool.Fori(0, NB - 1) as b:
                iteration(b, True)
            iteration(NB - 1, False)

            pool.wait_ge(pt_out, 16 * NB)
            pool.wait_ge(x2_out, 32 * NB)
            done = [0]
            for m, parts in enumerate(pieces):
                pool.wait_ge(raw_in[m % 3], raw_count[m])
                for n, part in enumerate(parts):
                    src, hi_dst, lo_dst = raw_part(m % 3, part), part[5], part[6]
                    nc.gpsimd.tensor_copy(hi_dst, src).then_inc(w_hi_ready, 1)
                    done[0] += 1
                    pool.wait_ge(w_hi_ready, done[0])
                    last = nc.gpsimd.tensor_tensor(lo_dst, src, hi_dst, ALU.subtract)
                last.then_inc(w_ready, 1)

            def residual(b):
                for m in range(TT * NH):
                    n, h = m // NH, m % NH
                    half = x2t[:, n % 2, h * HALF:(h + 1) * HALF]
                    if h == 0:
                        pool.wait_ge(x2t_in[n % 2], b * 32 + 16 * (n // 2) + 16)
                    pool.wait_ge(ffn_ready, b * 8 + m + 1)
                    nc.gpsimd.tensor_tensor(half, ffn[:, m % 2, :], half, ALU.add).then_inc(out_ready, 1)

            with pool.Fori(0, NB) as b:
                residual(b)


_NAMES = ["x", "w1", "w2t", "b2", "mask", "u1", "v1", "u2", "v2", "b1_main", "b1_tail", "b2f", "ct", "wmod"]


def kernel(**inputs):
    import numpy as np
    import concourse.bacc as bacc
    from concourse.bass_utils import run_bass_kernel_spmd as run

    def get(name):
        return np.asarray(inputs["L0_" + name])

    b1 = get("ffn_b1").reshape(2, -1)
    inter = b1.shape[1]
    whole = inter // P * P
    assert whole < inter
    laid = {
        "x": get("attn_x"),
        "w1": get("attn_w1"),
        "w2t": get("attn_w2").T,
        "b2": get("attn_b2").reshape(-1, P).T,
        "mask": get("attn_sparse_mask"),
        "u1": get("ffn_U1"),
        "v1": get("ffn_V1"),
        "u2": get("ffn_U2"),
        "v2": get("ffn_V2"),
        "b1_main": b1[:, :whole].reshape(2, -1, P).transpose(2, 1, 0),
        "b1_tail": b1[:, whole:].T.reshape(inter - whole, 1, 2),
        "b2f": get("ffn_b2").reshape(1, -1),
        "ct": get("c").T,
        "wmod": get("wmod"),
    }
    nc = bacc.Bacc("TRN2", target_bir_lowering=False, num_devices=1, dynamic_dma_scratch_size=1024)
    arrays, args = {}, []
    for name in _NAMES:
        a = np.ascontiguousarray(laid[name])
        arrays[f"in_{name}"] = a
        args.append(nc.dram_tensor(f"in_{name}", a.shape, mybir.dt.from_np(a.dtype), kind="ExternalInput").ap())
    out = nc.dram_tensor("out", laid["x"].shape, F32, kind="ExternalOutput").ap()
    adaln_block(nc, *args, out)
    result = run(nc, [arrays], core_ids=[0])
    return result.results[0]["out"]
```

```python
from contextlib import ExitStack

import concourse.bass as bass
from concourse import mybir

F32 = mybir.dt.float32
F32R = mybir.dt.float32r
I32 = mybir.dt.int32
ACT = mybir.ActivationFunctionType
ALU = mybir.AluOpType
AX = mybir.AxisListType

P = 128
EPS = 1e-5
GATE_FLOOR = 0.25


def adaln_block(nc, x, w1, w2t, b2, mask, u1, v1, u2, v2, b1_main, b1_tail, b2f, ct, wmod, out):
    NB, TOK, D = x.shape
    FB = D // P
    TT = TOK // P
    R = u1.shape[1]
    RB = R // P
    INTER = u2.shape[0]
    IB = -(-INTER // P)
    HALF = 512
    NH = D // HALF
    width = [min(P, INTER - P * i) for i in range(IB)]
    assert TOK == HALF and IB % 2 == 0 and NB % 2 == 0 and RB == 2

    BAND = 3 * P
    def band_cols(s):
        return max(0, P * (s - 1)), min(D, P * (s + 2))

    off_band = []
    for s in range(FB):
        lo_c, hi_c = band_cols(s)
        for a, e in ((0, lo_c), (hi_c, D)):
            while a < e:
                off_band.append((s, a, min(a + HALF, e)))
                a = min(a + HALF, e)

    SCALE1, BETA1, GA, SCALE2, BETA2 = 0, FB, 2 * FB, 3 * FB, 4 * FB
    NCOL = 4 * FB + RB

    x_tiles = x.rearrange("b (n p) d -> b p n d", p=P)
    out_tiles = out.rearrange("b (n p) d -> b n p d", p=P)
    x2_dram = nc.dram_tensor("x2_dram", [NB, TOK, D], F32, kind="Internal").ap()
    x2_store = x2_dram.rearrange("b (n p) d -> b p n d", p=P)
    x2_tiles = x2_dram.rearrange("b (n p) d -> b n p d", p=P)
    pt_dram = nc.dram_tensor("pt_dram", [NB, P, 2, RB, TOK], F32, kind="Internal").ap()
    gb_dram = nc.dram_tensor("gb_dram", [NB, 1, D], F32, kind="Internal").ap()

    with ExitStack() as ctx:
        def sem(name):
            return ctx.enter_context(nc.semaphore(name))

        def buf(scope, name, shape, dt=F32):
            return scope.enter_context(nc.sbuf_tensor(name, shape, dt))

        bank = ctx.enter_context(nc.psum_tensor("bank", [P, 8, HALF], F32))

        ident = buf(ctx, "ident", [P, P])
        table = buf(ctx, "table", [P, NB, NCOL])
        b1_sb = buf(ctx, "b1_sb", [P, IB, 2])
        b2_sb = buf(ctx, "b2_sb", [P, FB])
        minus_half = buf(ctx, "minus_half", [P, TT])
        tick = buf(ctx, "tick", [P, 1])
        off_any = buf(ctx, "off_any", [P, len(off_band)])
        off_max = buf(ctx, "off_max", [P, 1])
        dense_flag = buf(ctx, "dense_flag", [P, 1])
        c_sb = buf(ctx, "c_sb", [P, FB, NB])
        c_pad = buf(ctx, "c_pad", [P, FB, 32])
        mod_sum = buf(ctx, "mod_sum", [P, 4, NB])
        gate_sign = buf(ctx, "gate_sign", [P, 4, NB])
        gate_size = buf(ctx, "gate_size", [P, 4, NB])
        gate_big = buf(ctx, "gate_big", [P, 4, NB])
        gb_feat = buf(ctx, "gb_feat", [P, FB, NB])
        gb_rows = buf(ctx, "gb_rows", [FB * NB, P])
        bn1 = buf(ctx, "bn1", [P, TT, 2, 6])
        bn2 = buf(ctx, "bn2", [P, TT, 2, 6])
        mv1 = buf(ctx, "mv1", [P, TT, 2])
        mv2 = buf(ctx, "mv2", [P, TT, 2])
        ve1 = buf(ctx, "ve1", [P, TT])
        ve2 = buf(ctx, "ve2", [P, TT])
        rstd1 = buf(ctx, "rstd1", [P, TT])
        rstd2 = buf(ctx, "rstd2", [P, TT])
        now1 = buf(ctx, "now1", [P, FB])
        now_beta = buf(ctx, "now_beta", [P, FB])
        now_ga = buf(ctx, "now_ga", [P, FB])
        now2 = buf(ctx, "now2", [P, FB + RB])
        eps = buf(ctx, "eps", [P, TT])
        p01 = ctx.enter_context(ExitStack())
        attn_hi = buf(p01, "attn_hi", [P, FB, D], F32R)
        with ExitStack() as staging:
            masked = buf(staging, "masked", [P, FB, D])
        off_junk = masked[:, 0, 0:HALF]
        attn_lo = buf(p01, "attn_lo", [P, FB, D], F32R)
        sh = buf(p01, "sh", [P, 2, FB, NB])
        sh_hi = buf(p01, "sh_hi", [P, 2, FB, NB], F32R)
        sh_lo = buf(p01, "sh_lo", [P, 2, FB, NB], F32R)
        with ExitStack() as p0:
            w1_sb = buf(p0, "w1_sb", [P, FB, D])
            w2t_sb = buf(p0, "w2t_sb", [P, FB, D])
            mask_sb = buf(p0, "mask_sb", [P, FB, D])
            wm_sb = buf(p0, "wm_sb", [P, 3, FB, HALF])
        with ExitStack() as p1:
            xs = buf(p1, "xs", [P, TT, D])
            h1_hi = buf(p1, "h1_hi", [P, FB, TOK], F32R)
            h1_lo = buf(p1, "h1_lo", [P, FB, TOK], F32R)
            xr = buf(p1, "xr", [P, TT, D])
            nrm = buf(p1, "nrm", [P, TT, D])
            g = buf(p1, "g", [P, FB, TOK])
            h2_hi = buf(p1, "h2_hi", [P, FB, TOK], F32R)
            h2_lo = buf(p1, "h2_lo", [P, FB, TOK], F32R)
            u1_hi = buf(p1, "u1_hi", [P, FB, R], F32R)
            u1_lo = buf(p1, "u1_lo", [P, FB, R], F32R)
            pt_st = buf(p1, "pt_st", [P, 2, RB, TOK], F32R)
            beta_rows = pt_st[0:NB, 1].bitcast(F32)
            mod_rows = pt_st[:, 0].bitcast(F32)
        p01.close()
        p2 = ctx
        v1_hi = buf(p2, "v1_hi", [P, RB, 2 * INTER], F32R)
        v1_lo = buf(p2, "v1_lo", [P, RB, 2 * INTER], F32R)
        with ExitStack() as p2a:
            raw = buf(p2a, "raw", [P, 3, RB * HALF])
        x2t = buf(p2, "x2t", [P, 2, D])
        ffn = buf(p2, "ffn", [P, 2, HALF])
        pt = buf(p2, "pt", [P, 2, 2, RB, TOK], F32R)
        u2_hi = buf(p2, "u2_hi", [P, IB, R], F32R)
        u2_lo = buf(p2, "u2_lo", [P, IB, R], F32R)
        v2_hi = buf(p2, "v2_hi", [P, RB, D], F32R)
        v2_lo = buf(p2, "v2_lo", [P, RB, D], F32R)
        act = buf(p2, "act", [P, 2, TOK])
        act_hi = buf(p2, "act_hi", [P, 4, TOK], F32R)
        act_lo = buf(p2, "act_lo", [P, 4, TOK], F32R)
        z_hi = buf(p2, "z_hi", [P, RB, TOK], F32R)
        z_lo = buf(p2, "z_lo", [P, RB, TOK], F32R)
        gb_bc = buf(p2, "gb_bc", [P, D])
        b2f_bc = buf(p2, "b2f_bc", [P, D])

        const_in = sem("const_in")
        w_in = [sem(f"w_in{k}") for k in range(FB)]
        mask_in = sem("mask_in")
        wm_in = [sem(f"wm_in{i}") for i in range(4)]
        consts_made = sem("consts_made")
        zero_made = sem("zero_made")
        c_ready = sem("c_ready")
        dve_step = sem("dve_step")
        off_known = sem("off_known")
        flag_known = sem("flag_known")
        attn_mm = sem("attn_mm")
        masked_ready = sem("masked_ready")
        attn_hi_ready = sem("attn_hi_ready")
        attn_lo_ready = sem("attn_lo_ready")
        dn_mm = sem("dn_mm")
        dn_masked = sem("dn_masked")
        dn_hi = sem("dn_hi")
        dn_lo = sem("dn_lo")
        mod_mm = sem("mod_mm")
        mod_rows_ready = sem("mod_rows_ready")
        mod_turned = sem("mod_turned")
        mod_read = sem("mod_read")
        mod_placed = sem("mod_placed")
        sh_hi_ready = sem("sh_hi_ready")
        sh_lo_ready = sem("sh_lo_ready")
        gb_turned = sem("gb_turned")
        gb_ready = sem("gb_ready")
        gb_out = sem("gb_out")
        beta_mm = sem("beta_mm")
        beta_rows_ready = sem("beta_rows_ready")
        beta_turned = sem("beta_turned")
        table_ready = sem("table_ready")
        u1_in = sem("u1_in")
        u1_hi_ready = sem("u1_hi_ready")
        u1_ready = sem("u1_ready")
        xs_in = sem("xs_in")
        xs_first = sem("xs_first")
        xr_in = [sem("xr_in0"), sem("xr_in1")]
        x2_out = sem("x2_out")
        bn_done = sem("bn_done")
        mv1_ready = sem("mv1_ready")
        mv2_ready = sem("mv2_ready")
        ve_ready = sem("ve_ready")
        rstd1_ready = sem("rstd1_ready")
        rstd2_ready = sem("rstd2_ready")
        n1_ready = sem("n1_ready")
        n2_ready = sem("n2_ready")
        turned = sem("turned")
        hi_ready = sem("hi_ready")
        lo_ready = sem("lo_ready")
        now1_ready = sem("now1_ready")
        now_beta_ready = sem("now_beta_ready")
        now_ga_ready = sem("now_ga_ready")
        now2_ready = sem("now2_ready")
        y_done = sem("y_done")
        gelu_done = sem("gelu_done")
        g_ready = sem("g_ready")
        back_done = sem("back_done")
        x2_ready = sem("x2_ready")
        p_done = sem("p_done")
        pt_hi_ready = sem("pt_hi_ready")
        pt_lo_ready = sem("pt_lo_ready")
        pt_out = sem("pt_out")
        raw_in = [sem(f"raw_in{i}") for i in range(3)]
        w_hi_ready = sem("w_hi_ready")
        w_ready = sem("w_ready")
        pt_in = [sem("pt_in0"), sem("pt_in1")]
        gate_done = sem("gate_done")
        up_done = sem("up_done")
        silu_done = sem("silu_done")
        act_done = sem("act_done")
        act_hi_ready = sem("act_hi_ready")
        act_lo_ready = sem("act_lo_ready")
        z_step = sem("z_step")
        z_hi_ready = sem("z_hi_ready")
        z_lo_ready = sem("z_lo_ready")
        o_mm = sem("o_mm")
        ffn_sum = sem("ffn_sum")
        ffn_ready = sem("ffn_ready")
        out_ready = sem("out_ready")
        b2f_in = sem("b2f_in")
        gb_in = sem("gb_in")
        x2t_in = [sem("x2t_in0"), sem("x2t_in1")]
        out_stored = sem("out_stored")

        NCHUNK = wmod.shape[1] // HALF
        wm_view = wmod.rearrange("(k p) n -> p k n", p=P)
        SA, CA, GA_KIND, SB, CB, GB_KIND = range(6)
        KINDS = [CA, SA, GA_KIND, CB, SB, GB_KIND]
        WM_PLACE = [0, 1, 2, 0, 1, 0, 1, 0, 1, 0, 3, 3]

        def chunk_cols(q):
            return slice(KINDS[q // 2] * D + q % 2 * HALF, KINDS[q // 2] * D + (q % 2 + 1) * HALF)

        late_chunk = xs[:].rearrange("p n d -> p (n d)").rearrange("p (k c) -> p k c", k=FB)

        def wm_chunk(q):
            return late_chunk if WM_PLACE[q] == 3 else wm_sb[:, WM_PLACE[q]]

        def before(q):
            return [c for c in range(q) if WM_PLACE[c] == WM_PLACE[q]]

        BACK_LAG, T1_LAG = 1, 2

        def at_start(b, early=True):
            return isinstance(b, int) and b == 0 and early

        def turn1(b):
            return 0 if isinstance(b, int) and b == 0 else b * 16 - 8

        def turn2(b):
            return b * 16 + (8 if isinstance(b, int) and b == NB - 1 else 16)

        GROUPS = [(a, min(a + HALF, INTER)) for a in range(0, INTER, HALF)]
        v1_view = v1.rearrange("(k p) f -> p k f", p=P)
        v2_view = v2.rearrange("(k p) f -> p k f", p=P)
        pieces = []
        piece_of = {}
        for q, (a, e) in enumerate(GROUPS):
            for name, base in (("gate", 0), ("up", INTER)):
                n = e - a
                pieces.append([(v1_view[:, :, base + a:base + e], P, RB, n, 0,
                                v1_hi[:, :, base + a:base + e], v1_lo[:, :, base + a:base + e])])
                piece_of[name, q] = len(pieces)
            full, rest = (e - a) // P, (e - a) % P
            i0 = a // P
            parts = [(u2[a:a + full * P, :].rearrange("(i p) r -> p i r", p=P), P, full, R, 0,
                      u2_hi[:, i0:i0 + full, :], u2_lo[:, i0:i0 + full, :])]
            if rest:
                parts.append((u2[a + full * P:e, :].rearrange("(i p) r -> p i r", i=1), rest, 1, R, full * R,
                              u2_hi[0:rest, i0 + full:i0 + full + 1, :],
                              u2_lo[0:rest, i0 + full:i0 + full + 1, :]))
            pieces.append(parts)
            piece_of["u2", q] = len(pieces)
        for h in range(NH):
            pieces.append([(v2_view[:, :, h * HALF:(h + 1) * HALF], P, RB, HALF, 0,
                            v2_hi[:, :, h * HALF:(h + 1) * HALF], v2_lo[:, :, h * HALF:(h + 1) * HALF])])
        PIECES = len(pieces)

        def raw_part(slot, part):
            _, rows, blocks, n, off, _, _ = part
            return raw[0:rows, slot, off:off + blocks * n].rearrange("p (k n) -> p k n", k=blocks)

        raw_count = []
        seen = [0, 0, 0]
        for m, parts in enumerate(pieces):
            seen[m % 3] += 16 * len(parts)
            raw_count.append(seen[m % 3])

        BAND_ORDER = [6, 7] + list(range(6))

        block = ctx.enter_context(nc.Block())

        @block.sync
        def _(sp):
            sp.dma_start(c_sb[:], ct.rearrange("(k p) b -> p k b", p=P)).then_inc(const_in, 16)
            sp.dma_start(b2_sb[:], b2[:, :]).then_inc(const_in, 16)
            sp.dma_start(b1_sb[:, 0:IB - 1, :], b1_main[:, :, :]).then_inc(const_in, 16)
            sp.dma_start(b1_sb[0:width[-1], IB - 1:IB, :], b1_tail[:, :, :]).then_inc(const_in, 16)
            for k in range(FB):
                rows = slice(k * P, (k + 1) * P)
                sp.dma_start(w1_sb[:, k, :], w1[rows, :]).then_inc(w_in[k], 16)
                sp.dma_start(w2t_sb[:, k, :], w2t[rows, :]).then_inc(w_in[k], 16)
            sp.dma_start(mask_sb[:], mask.rearrange("(k p) t -> p k t", p=P)).then_inc(mask_in, 16)

            def wm_load(q):
                if before(q):
                    sp.wait_ge(mod_mm, before(q)[-1] + 1)
                sp.dma_start(wm_chunk(q), wm_view[:, :, chunk_cols(q)]).then_inc(wm_in[WM_PLACE[q]], 16)

            for q in range(2):
                wm_load(q)
            sp.wait_ge(mod_mm, 1)
            sp.dma_start(xs[:, 0:TT // 2, :], x_tiles[0, :, 0:TT // 2, :]).then_inc(xs_first, 16)
            sp.dma_start(xs[:, TT // 2:TT, :], x_tiles[0, :, TT // 2:TT, :]).then_inc(xs_in, 16)
            for q in range(2, 4):
                wm_load(q)
            u1_raw = xr[:, 0:2, :].rearrange("p n d -> p (n d)").rearrange("p (k r) -> p k r", k=FB)
            sp.dma_start(u1_raw, u1.rearrange("(k p) r -> p k r", p=P)).then_inc(u1_in, 16)
            for q in range(4, 6):
                wm_load(q)
            sp.wait_ge(n1_ready, 4)
            sp.dma_start(xs[:], x_tiles[1]).then_inc(xs_in, 16)

            def raw_load(m):
                if m >= 3:
                    sp.wait_ge(w_ready, m - 2)
                for part in pieces[m]:
                    sp.dma_start(raw_part(m % 3, part), part[0]).then_inc(raw_in[m % 3], 16)

            def iteration(b, has_y, has_prev, has_load, chunks=(), weights=False):
                if has_y:
                    if has_prev:
                        sp.wait_ge(x2_out, b * 32)
                    else:
                        sp.wait_ge(u1_ready, 1)
                    for half in range(2):
                        n = slice(half * TT // 2, (half + 1) * TT // 2)
                        sp.dma_start(xr[:, n, :], x_tiles[b, :, n, :]).then_inc(xr_in[half], 16)
                for q in chunks:
                    if q == NCHUNK - 2:
                        sp.wait_ge(n1_ready, NB * 4)
                    wm_load(q)
                if has_load:
                    sp.wait_ge(n1_ready, b * 4 + 8)
                    sp.dma_start(xs[:], x_tiles[b + 2]).then_inc(xs_in, 16)
                if at_start(b):
                    wm_load(8)
                    wm_load(9)
                if has_y:
                    sp.wait_ge(x2_ready, b * 8 + 4)
                    sp.dma_start(x2_store[b, :, 0:TT // 2, :], xr[:, 0:TT // 2, :]).then_inc(x2_out, 16)
                if has_prev:
                    sp.wait_ge(pt_lo_ready, b * 2)
                    sp.dma_start(pt_dram[b - 1], pt_st[:].bitcast(F32)).then_inc(pt_out, 16)
                if weights:
                    sp.wait_ge(y_done, FB * NB)
                    sp.dma_start(pt[:, 0].bitcast(F32), pt_dram[0]).then_inc(pt_in[0], 16)
                    for m in range(3):
                        raw_load(m)
                if has_y:
                    sp.wait_ge(n2_ready, b * 4 + 4)
                    sp.dma_start(x2_store[b, :, TT // 2:TT, :], xr[:, TT // 2:TT, :]).then_inc(x2_out, 16)
                if weights:
                    for m in range(3, 5):
                        raw_load(m)

            iteration(0, True, False, True, (6, 7))
            with sp.Fori(1, NB - 2) as b:
                iteration(b, True, True, True)
            iteration(NB - 2, True, True, False, (10,))
            iteration(NB - 1, True, True, False, (11,), True)
            sp.wait_ge(pt_lo_ready, 2 * NB)
            sp.dma_start(pt_dram[NB - 1], pt_st[:].bitcast(F32)).then_inc(pt_out, 16)
            sp.wait_ge(gb_ready, 1)
            for k in range(FB):
                sp.dma_start(gb_dram[:, 0, k * P:(k + 1) * P], gb_rows[k * NB:(k + 1) * NB, :]).then_inc(gb_out, 16)

            for m in range(5, PIECES):
                raw_load(m)
                if m == 6:
                    sp.wait_ge(x2_out, 32 * NB)
                    sp.dma_start(pt[:, 1].bitcast(F32), pt_dram[1]).then_inc(pt_in[1], 16)
            sp.wait_ge(pt_out, 16 * NB)
            sp.wait_ge(gb_out, 16 * FB)
            sp.dma_start(b2f_bc[:], b2f[:, :].broadcast_to([P, D])).then_inc(b2f_in, 16)
            sp.wait_ge(w_ready, PIECES)

            def tile_in(b, n):
                sp.dma_start(x2t[:, n % 2, :], x2_tiles[b, n]).then_inc(x2t_in[n % 2], 16)

            def batch(b, q, last):
                if not last and not at_start(b):
                    sp.wait_ge(up_done, b * IB)
                    sp.dma_start(pt[:, 1 - q].bitcast(F32), pt_dram[b + 1]).then_inc(pt_in[1 - q], 16)
                if not at_start(b):
                    sp.wait_ge(ffn_ready, b * 8)
                sp.dma_start(gb_bc[:], gb_dram[b].broadcast_to([P, D])).then_inc(gb_in, 16)
                for n in range(TT):
                    sp.wait_ge(out_ready, b * 8 + 2 * n + 2)
                    sp.dma_start(out_tiles[b, n], x2t[:, n % 2, :]).then_inc(out_stored, 16)
                    sp.wait_ge(out_stored, b * 64 + 16 * n + 16)
                    if n < 2:
                        tile_in(b, n + 2)
                    elif not last:
                        tile_in(b + 1, n - 2)

            tile_in(0, 0)
            tile_in(0, 1)
            batch(0, 0, False)
            with sp.Fori(1, NB // 2) as i:
                batch(i * 2 - 1, 1, False)
                batch(i * 2, 0, False)
            batch(NB - 1, 1, True)
            sp.wait_ge(out_stored, 64 * NB)

        @block.tensor
        def _(pe):
            def three(acc, s_hi, s_lo, m_hi, m_lo, start, stop):
                nc.tensor.matmul(acc, s_hi, m_hi, start=start, stop=False)
                nc.tensor.matmul(acc, s_hi, m_lo, start=False, stop=False)
                return nc.tensor.matmul(acc, s_lo, m_hi, start=False, stop=stop)

            def attn_product(acc, s, a, e):
                for k in range(FB):
                    last = nc.tensor.matmul(acc, w1_sb[:, k, s * P:(s + 1) * P], w2t_sb[:, k, a:e],
                                            start=(k == 0), stop=(k == FB - 1))
                return last

            for k in range(FB):
                pe.wait_ge(w_in[k], 32)
                for s in BAND_ORDER:
                    a, e = band_cols(s)
                    last = nc.tensor.matmul(bank[:, s, 0:e - a], w1_sb[:, k, s * P:(s + 1) * P], w2t_sb[:, k, a:e],
                                            start=(k == 0), stop=(k == FB - 1))
                    if k == FB - 1:
                        last.then_inc(attn_mm, 1)
            pe.wait_ge(flag_known, 1)
            dense = nc.tensor.value_load(dense_flag[0:1, 0:1].bitcast(I32))
            with nc.tensor.If(dense != 0):
                pe.wait_ge(masked_ready, FB)
                for n, (s, a, e) in enumerate(off_band):
                    if n >= 2:
                        pe.wait_ge(dn_masked, n - 1)
                    attn_product(bank[:, n % 2, 0:e - a], s, a, e).then_inc(dn_mm, 1)

            def mod_product(q, rows_bank):
                pe.wait_ge(wm_in[WM_PLACE[q]], 16 * len(before(q)) + 16)
                if q >= 2:
                    pe.wait_ge(mod_rows_ready, q - 1)
                for k in range(FB):
                    j = k % 4
                    last = nc.tensor.matmul(bank[32 * j:32 * j + 32, rows_bank, :], c_pad[:, k, :],
                                            wm_chunk(q)[:, k, :], start=(k < 4), stop=(k >= 4),
                                            skip_group_check=True)
                last.then_inc(mod_mm, 1)

            def mod_turn(q, turn_bank):
                pe.wait_ge(mod_rows_ready, q + 1)
                if q >= 2:
                    pe.wait_ge(mod_read, q - 1)
                for j in range(4):
                    cols = slice(j * P, (j + 1) * P)
                    last = nc.tensor.transpose(bank[:, turn_bank, cols], mod_rows[:, q % 2, cols], ident[:])
                last.then_inc(mod_turned, 1)

            def mod_pair(q):
                mod_product(q, 6)
                mod_product(q + 1, 7)
                mod_turn(q, 4)
                mod_turn(q + 1, 5)

            pe.wait_ge(consts_made, 1)
            pe.wait_ge(c_ready, 1)
            pe.wait_ge(masked_ready, 2)
            mod_product(0, 6)
            mod_product(1, 7)
            pe.wait_ge(masked_ready, FB)
            mod_turn(0, 4)
            mod_turn(1, 5)

            def turn(number, k):
                if not (isinstance(number, int) and number < 2):
                    pe.wait_ge(lo_ready, number - 1)
                for n in range(TT):
                    last = nc.tensor.transpose(bank[:, 2 + k % 2, n * P:(n + 1) * P],
                                               nrm[:, n, k * P:(k + 1) * P], ident[:])
                last.then_inc(turned, 1)

            pe.wait_ge(n1_ready, 4)
            for k in range(FB):
                turn(k, k)
                if k == 1:
                    mod_product(2, 6)
                elif k == 3:
                    mod_product(3, 7)
                elif k == 5:
                    mod_turn(2, 4)
            mod_turn(3, 5)

            def shift_product(v, acc, w_hi, w_lo, s, start, stop):
                nc.tensor.matmul(acc, sh_hi[:, v, s, :], w_hi, start=start, stop=False, skip_group_check=True)
                nc.tensor.matmul(acc, sh_hi[:, v, s, :], w_lo, start=False, stop=False, skip_group_check=True)
                return nc.tensor.matmul(acc, sh_lo[:, v, s, :], w_hi, start=False, stop=stop, skip_group_check=True)

            def attn_shift(s, a, e, start, stop):
                h = a // HALF
                return shift_product(0, bank[0:NB, h, a - h * HALF:e - h * HALF], attn_hi[:, s, a:e],
                                     attn_lo[:, s, a:e], s, start, stop)

            def by_bank(parts):
                return [(s, max(a, h * HALF), min(e, (h + 1) * HALF)) for h in range(NH) for s, a, e in parts
                        if max(a, h * HALF) < min(e, (h + 1) * HALF)]

            pe.wait_ge(sh_lo_ready, 1)
            pe.wait_ge(attn_lo_ready, FB)
            near = by_bank([(s, *band_cols(s)) for s in range(FB)])
            for h in range(NH):
                of_bank = [part for part in near if part[1] // HALF == h]
                for part in of_bank[:-1]:
                    attn_shift(*part, part == of_bank[0], False)
            with nc.tensor.If(dense != 0):
                pe.wait_ge(dn_lo, len(off_band))
                for part in by_bank(off_band):
                    attn_shift(*part, False, False)
            for h in range(NH):
                part = [part for part in near if part[1] // HALF == h][-1]
                last = attn_shift(*part, False, True)
            last.then_inc(beta_mm, 1)

            def beta2_product():
                pe.wait_ge(sh_lo_ready, 2)
                pe.wait_ge(u1_ready, 1)
                for k in range(FB):
                    last = shift_product(1, bank[0:NB, 6, 0:R], u1_hi[:, k, :], u1_lo[:, k, :], k,
                                         k == 0, k == FB - 1)
                last.then_inc(beta_mm, 1)

            def beta_turn(v, turn_bank, blocks):
                pe.wait_ge(beta_rows_ready, v + 1)
                for t in range(blocks):
                    last = nc.tensor.transpose(bank[:, turn_bank, t * NB:(t + 1) * NB],
                                               beta_rows[:, t // 4, t % 4 * P:(t % 4 + 1) * P], ident[0:NB, 0:NB])
                last.then_inc(beta_turned, 1)

            mod_pair(4)
            beta_turn(0, 2, FB)

            def y(b, t):
                first = turn1(b)
                if not at_start(b, t < 2):
                    pe.wait_ge(gelu_done, b * 8 + t - 1)
                elif t == 0:
                    pe.wait_ge(beta_rows_ready, 1)
                pe.wait_ge(lo_ready, first + min(t + 2, FB))
                near = [s for s in range(FB) if abs(s - t) <= 1]
                far = [s for s in range(FB) if abs(s - t) > 1]
                acc = bank[:, t % 2, :]
                cols = slice(t * P, (t + 1) * P)
                for s in near[:-1]:
                    three(acc, attn_hi[:, s, cols], attn_lo[:, s, cols], h1_hi[:, s, :], h1_lo[:, s, :],
                          s == near[0], False)
                with nc.tensor.If(dense != 0):
                    pe.wait_ge(lo_ready, first + FB)
                    for s in far:
                        three(acc, attn_hi[:, s, cols], attn_lo[:, s, cols], h1_hi[:, s, :], h1_lo[:, s, :],
                              False, False)
                s = near[-1]
                three(acc, attn_hi[:, s, cols], attn_lo[:, s, cols], h1_hi[:, s, :], h1_lo[:, s, :],
                      False, True).then_inc(y_done, 1)

            def turn_back(b, k):
                if not at_start(b, k < 2):
                    pe.wait_ge(x2_ready, b * 8 + k - 1)
                if k == 0:
                    pe.wait_ge(g_ready, b * 8 + 8)
                    if at_start(b):
                        pe.wait_ge(mod_read, 6)
                n = k // 2
                for j in range(4):
                    last = nc.tensor.transpose(bank[:, 4 + k % 2, j * P:(j + 1) * P],
                                               g[:, 4 * (k % 2) + j, n * P:(n + 1) * P], ident[:])
                last.then_inc(back_done, 1)

            def p_product(b, k):
                pe.wait_ge(lo_ready, turn2(b) + k + 1)
                if k == 0 and not at_start(b):
                    pe.wait_ge(pt_lo_ready, b * 2)
                for r in range(RB):
                    cols = slice(r * P, (r + 1) * P)
                    last = three(bank[:, 6 + r, :], u1_hi[:, k, cols], u1_lo[:, k, cols],
                                 h2_hi[:, k, :], h2_lo[:, k, :], k == 0, k == FB - 1)
                if k == FB - 1:
                    last.then_inc(p_done, 1)

            def iteration(b, has_y, has_prev, has_next):
                for t in range(FB):
                    if has_y:
                        y(b, t)
                    if at_start(b - 1, t == 1):
                        beta_turn(1, 7, RB)
                    if not has_next and has_y and t in (2, FB - 1):
                        if t == 2:
                            pe.wait_ge(x2_ready, b * 8)
                        q = 10 if t == 2 else 11
                        mod_product(q, 4)
                        mod_turn(q, 5)
                        if t == FB - 1:
                            pe.wait_ge(mod_read, NCHUNK)
                    if has_prev and 3 <= t <= 6:
                        if t == 3:
                            pe.wait_ge(n2_ready, b * 4)
                        for k in (2 * (t - 3), 2 * (t - 3) + 1):
                            turn(turn2(b - 1) + k, k)
                if at_start(b):
                    mod_product(6, 6)
                    mod_product(7, 7)
                    pe.wait_ge(gelu_done, FB)
                    mod_turn(6, 0)
                    mod_turn(7, 1)
                for step in range(FB + T1_LAG):
                    if has_prev and step < FB:
                        if at_start(b - 1, step == 0):
                            pe.wait_ge(table_ready, 2)
                        p_product(b - 1, step)
                    if has_y and BACK_LAG <= step < FB + BACK_LAG:
                        turn_back(b, step - BACK_LAG)
                    if has_next and step >= T1_LAG:
                        k = step - T1_LAG
                        if k == 0:
                            pe.wait_ge(n1_ready, b * 4 + 8)
                        turn(turn1(b + 1) + k, k)
                if at_start(b):
                    pe.wait_ge(x2_ready, FB)
                    mod_pair(8)
                    pe.wait_ge(mod_placed, 10)
                    beta2_product()

            iteration(0, True, False, True)
            iteration(1, True, True, True)
            with pe.Fori(2, NB - 1) as b:
                iteration(b, True, True, True)
            iteration(NB - 1, True, True, False)
            pe.wait_ge(x2_ready, FB * NB)
            pe.wait_ge(mod_placed, NCHUNK)
            nc.tensor.transpose(bank[0:FB * NB, 4, 0:P], gb_feat[:].rearrange("p k b -> p (k b)"),
                                ident[:]).then_inc(gb_turned, 1)
            iteration(NB, False, True, False)

            def h_product(b, q, i):
                if i == 0:
                    pe.wait_ge(pt_in[q], (b - q) * 8 + 16)
                if not at_start(b, i < 2):
                    pe.wait_ge(act_done, b * IB + i - 1)
                w = width[i]
                for name, first_bank, base, done in (("gate", 0, 0, gate_done), ("up", 2, INTER, up_done)):
                    if i % 4 == 0:
                        pe.wait_ge(w_ready, piece_of[name, i // 4])
                    cols = slice(base + i * P, base + i * P + w)
                    for r in range(RB):
                        last = three(bank[0:w, first_bank + i % 2, :], v1_hi[:, r, cols], v1_lo[:, r, cols],
                                     pt[:, q, 0, r, :], pt[:, q, 1, r, :], r == 0, r == RB - 1)
                    last.then_inc(done, 1)

            def z_product(b, q, i):
                pe.wait_ge(act_lo_ready, b * IB + i + 1)
                if i % 4 == 0:
                    pe.wait_ge(w_ready, piece_of["u2", i // 4])
                if at_start(b, i == 0):
                    pe.wait_ge(gb_ready, 1)
                elif i == 0:
                    pe.wait_ge(z_lo_ready, b * 2)
                w = width[i]
                slot = (q * IB + i) % 4
                for r in range(RB):
                    cols = slice(r * P, (r + 1) * P)
                    last = three(bank[:, 4 + r, :], u2_hi[0:w, i, cols], u2_lo[0:w, i, cols],
                                 act_hi[0:w, slot, :], act_lo[0:w, slot, :], i == 0, i == IB - 1)
                last.then_inc(z_step, 1)

            def out_product(b):
                pe.wait_ge(z_lo_ready, b * 2 + 2)
                pe.wait_ge(w_ready, PIECES)
                if at_start(b):
                    pe.wait_ge(pt_lo_ready, 2 * NB)
                for m in range(TT * NH):
                    n, h = m // NH, m % NH
                    if not at_start(b, m < 2):
                        pe.wait_ge(ffn_sum, b * 8 + max(m - 1, 0))
                    toks, cols = slice(n * P, (n + 1) * P), slice(h * HALF, (h + 1) * HALF)
                    for r in range(RB):
                        last = three(bank[:, 6 + m % 2, :], z_hi[:, r, toks], z_lo[:, r, toks],
                                     v2_hi[:, r, cols], v2_lo[:, r, cols], r == 0, r == RB - 1)
                    last.then_inc(o_mm, 1)

            def batch(b, q, last):
                for i in range(2, IB):
                    h_product(b, q, i)
                    z_product(b, q, i - 2)
                if not last:
                    h_product(b + 1, 1 - q, 0)
                z_product(b, q, IB - 2)
                z_product(b, q, IB - 1)
                if not last:
                    h_product(b + 1, 1 - q, 1)
                out_product(b)

            pe.wait_ge(gelu_done, 8 * NB)
            pe.wait_ge(x2_ready, 8 * NB)
            pe.wait_ge(lo_ready, turn2(NB - 1) + FB)
            h_product(0, 0, 0)
            h_product(0, 0, 1)
            batch(0, 0, False)
            with pe.Fori(1, NB // 2) as i:
                batch(i * 2 - 1, 1, False)
                batch(i * 2, 0, False)
            batch(NB - 1, 1, True)

        @block.scalar
        def _(ae):
            ae.wait_ge(const_in, 64)
            ae.wait_ge(zero_made, 1)
            nc.scalar.activation(c_pad[:, :, 0:NB], c_sb[:], ACT.Silu).then_inc(c_ready, 1)
            for n, s in enumerate(BAND_ORDER):
                a, e = band_cols(s)
                ae.wait_ge(masked_ready, n + 1)
                nc.scalar.activation(attn_hi[:, s, a:e], masked[:, s, a:e],
                                     ACT.Copy).then_inc(attn_hi_ready, 1)
            ae.wait_ge(flag_known, 1)
            dense = nc.scalar.value_load(dense_flag[0:1, 0:1].bitcast(I32))
            with nc.scalar.If(dense != 0):
                for n, (s, a, e) in enumerate(off_band):
                    ae.wait_ge(dn_masked, n + 1)
                    nc.scalar.activation(attn_hi[:, s, a:e], masked[:, s, a:e],
                                         ACT.Copy).then_inc(dn_hi, 1)

            def shift_hi(v):
                ae.wait_ge(mod_placed, (4, 10)[v])
                nc.scalar.activation(sh_hi[:, v], sh[:, v], ACT.Copy).then_inc(sh_hi_ready, 1)

            def hi(number, k, h_hi, scale):
                ae.wait_ge(turned, number + k + 1)
                nc.scalar.activation(h_hi[:, k, :], bank[:, 2 + k % 2, :], ACT.Copy,
                                     scale=scale[:, k:k + 1]).then_inc(hi_ready, 1)

            def gelu(b, t):
                ae.wait_ge(y_done, b * 8 + t + 1)
                nc.scalar.activation(g[:, t, :], bank[:, t % 2, :], ACT.Gelu,
                                     bias=now_beta[:, t:t + 1]).then_inc(gelu_done, 1)

            def load_now1(b):
                if not at_start(b):
                    ae.wait_ge(lo_ready, turn1(b - 1) + FB)
                    ae.wait_ge(y_done, b * 8)
                nc.scalar.activation(now1[:], table[:, b, SCALE1:SCALE1 + FB], ACT.Copy).then_inc(now1_ready, 1)
                ae.wait_ge(now1_ready, b + 1)

            def iteration(b, has_y, has_prev, has_next):
                def load_ga():
                    nc.scalar.activation(now_ga[:], table[:, b, GA:GA + FB], ACT.Copy).then_inc(now_ga_ready, 1)

                if has_y:
                    if not has_prev:
                        ae.wait_ge(table_ready, 1)
                    else:
                        ae.wait_ge(back_done, b * 8)
                    nc.scalar.activation(now_beta[:], table[:, b, BETA1:BETA1 + FB],
                                         ACT.Copy).then_inc(now_beta_ready, 1)
                    if has_prev:
                        load_ga()
                    ae.wait_ge(now_beta_ready, b + 1)
                for t in range(FB):
                    if has_y:
                        gelu(b, t)
                    if has_y and not has_prev and t == 3:
                        ae.wait_ge(mod_placed, 6)
                        load_ga()
                    if has_prev and 3 <= t <= 6:
                        if t == 3:
                            ae.wait_ge(table_ready, 2)
                            if not at_start(b - 1):
                                ae.wait_ge(pt_lo_ready, b * 2 - 2)
                            nc.scalar.activation(now2[:], table[:, b - 1, SCALE2:SCALE2 + FB + RB],
                                                 ACT.Copy).then_inc(now2_ready, 1)
                            ae.wait_ge(now2_ready, b)
                        for k in (2 * (t - 3), 2 * (t - 3) + 1):
                            hi(turn2(b - 1), k, h2_hi, now2)
                if has_next:
                    load_now1(b + 1)
                for step in range(FB + T1_LAG):
                    if has_next and step >= T1_LAG:
                        hi(turn1(b + 1), step - T1_LAG, h1_hi, now1)
                    if has_prev and step == FB:
                        ae.wait_ge(p_done, b)
                        if not at_start(b - 1):
                            ae.wait_ge(pt_out, b * 16 - 16)
                        for r in range(RB):
                            nc.scalar.activation(pt_st[:, 0, r, :], bank[:, 6 + r, :], ACT.Identity,
                                                 bias=now2[:, FB + r:FB + r + 1]).then_inc(pt_hi_ready, 1)

            ae.wait_ge(mod_placed, 2)
            load_now1(0)
            for k in range(FB):
                hi(0, k, h1_hi, now1)
            shift_hi(0)
            iteration(0, True, False, True)
            shift_hi(1)
            iteration(1, True, True, True)
            with ae.Fori(2, NB - 1) as b:
                iteration(b, True, True, True)
            iteration(NB - 1, True, True, False)
            iteration(NB, False, True, False)

            def silu(b, q, i):
                w = width[i]
                ae.wait_ge(gate_done, b * IB + i + 1)
                if not at_start(b, i < 2):
                    ae.wait_ge(act_lo_ready, b * IB + i - 1)
                nc.scalar.activation(act[0:w, i % 2, :], bank[0:w, i % 2, :], ACT.Silu,
                                     bias=b1_sb[0:w, i, 0:1]).then_inc(silu_done, 1)

            def act_hi_part(b, q, i):
                w = width[i]
                slot = (q * IB + i) % 4
                ae.wait_ge(act_done, b * IB + i + 1)
                if not at_start(b, i < 4):
                    ae.wait_ge(z_step, b * IB + max(i - 3, 0))
                nc.scalar.activation(act_hi[0:w, slot, :], act[0:w, i % 2, :], ACT.Copy).then_inc(act_hi_ready, 1)

            def batch(b, q, last):
                for i in range(1, IB):
                    silu(b, q, i)
                    act_hi_part(b, q, i - 1)
                if not last:
                    silu(b + 1, 1 - q, 0)
                act_hi_part(b, q, IB - 1)
                ae.wait_ge(z_step, b * IB + IB)
                if not at_start(b):
                    ae.wait_ge(o_mm, b * 8)
                for r in range(RB):
                    nc.scalar.activation(z_hi[:, r, :], bank[:, 4 + r, :], ACT.Copy).then_inc(z_hi_ready, 1)

            silu(0, 0, 0)
            batch(0, 0, False)
            with ae.Fori(1, NB // 2) as i:
                batch(i * 2 - 1, 1, False)
                batch(i * 2, 0, False)
            batch(NB - 1, 1, True)

        @block.vector
        def _(dve):
            steps = [0]

            def link(ins):
                steps[0] += 1
                ins.then_inc(dve_step, 1)
                dve.wait_ge(dve_step, steps[0])

            dve.wait_ge(mask_in, 16)
            for n, (s, a, e) in enumerate(off_band):
                link(nc.vector.tensor_scalar(off_junk[:, 0:e - a], mask_sb[:, s, a:e], 0.0, 0.0, ALU.not_equal,
                                             ALU.max, accum_out=off_any[:, n:n + 1]))
            nc.vector.tensor_reduce(off_max[:], off_any[:], AX.X, ALU.max).then_inc(off_known, 1)

            def mask_product(src_bank, s, a, e, ready):
                nc.vector.tensor_tensor(masked[:, s, a:e], bank[:, src_bank, 0:e - a], mask_sb[:, s, a:e],
                                        ALU.mult).then_inc(ready, 1)

            def attn_rest(s, a, e, ready):
                nc.vector.tensor_tensor(attn_lo[:, s, a:e], masked[:, s, a:e], attn_hi[:, s, a:e],
                                        ALU.subtract).then_inc(ready, 1)

            for n, s in enumerate(BAND_ORDER):
                dve.wait_ge(attn_mm, n + 1)
                mask_product(s, s, *band_cols(s), masked_ready)
            for n, s in enumerate(BAND_ORDER):
                dve.wait_ge(attn_hi_ready, n + 1)
                attn_rest(s, *band_cols(s), attn_lo_ready)
            dve.wait_ge(flag_known, 1)
            dense = nc.vector.value_load(dense_flag[0:1, 0:1].bitcast(I32))
            with nc.vector.If(dense != 0):
                dve.wait_ge(attn_lo_ready, FB)
                for n, (s, a, e) in enumerate(off_band):
                    dve.wait_ge(dn_mm, n + 1)
                    mask_product(n % 2, s, a, e, dn_masked)
                    dve.wait_ge(dn_hi, n + 1)
                    attn_rest(s, a, e, dn_lo)

            def clamp_gate(dst):
                v = mod_sum[:]
                nc.vector.tensor_scalar(gate_sign[:], v, 0.0, 2.0, ALU.is_ge, ALU.mult)
                link(nc.vector.scalar_tensor_tensor(gate_size[:], v, -1.0, v, ALU.mult, ALU.max))
                link(nc.vector.tensor_scalar(gate_big[:], gate_size[:], GATE_FLOOR, None, ALU.max))
                return nc.vector.scalar_tensor_tensor(dst, gate_sign[:], -1.0, gate_big[:], ALU.add, ALU.mult)

            def mod_copy(q, rows_bank):
                dve.wait_ge(mod_mm, q + 1)
                if q >= 2:
                    dve.wait_ge(mod_turned, q - 1)
                nc.vector.tensor_copy(mod_rows[:, q % 2, :], bank[:, rows_bank, :]).then_inc(mod_rows_ready, 1)

            def mod_place(q, turn_bank):
                kind, j0 = KINDS[q // 2], q % 2 * 4
                dve.wait_ge(mod_turned, q + 1)
                if q >= 1:
                    dve.wait_ge(mod_placed, q)
                parts = bank[:, turn_bank, :].rearrange("p (k j c) -> p k c j", k=4, j=4)[:, :, 0:NB, :]
                nc.vector.tensor_reduce(mod_sum[:], parts, AX.X, ALU.add).then_inc(mod_read, 1)
                dve.wait_ge(mod_read, q + 1)
                if kind in (SA, SB):
                    last = nc.vector.tensor_copy(sh[:, kind // 3, j0:j0 + 4, :], mod_sum[:])
                elif kind in (CA, CB):
                    base = {CA: SCALE1, CB: SCALE2}[kind] + j0
                    last = nc.vector.tensor_scalar(table[:, :, base:base + 4].rearrange("p b j -> p j b"), mod_sum[:],
                                                   1.0, None, ALU.add)
                elif kind == GA_KIND:
                    last = clamp_gate(table[:, :, GA + j0:GA + j0 + 4].rearrange("p b j -> p j b"))
                else:
                    last = clamp_gate(gb_feat[:, j0:j0 + 4, :])
                last.then_inc(mod_placed, 1)

            def mod_pair(q):
                mod_copy(q, 6)
                mod_copy(q + 1, 7)
                mod_place(q, 4)
                mod_place(q + 1, 5)

            def shift_lo(v):
                dve.wait_ge(sh_hi_ready, v + 1)
                nc.vector.tensor_tensor(sh_lo[:, v], sh[:, v], sh_hi[:, v], ALU.subtract).then_inc(sh_lo_ready, 1)

            def stats1(b, halves):
                for m in halves:
                    if at_start(b, m == 0):
                        dve.wait_ge(xs_first, 16)
                    if m == (TT if at_start(b) else 0):
                        dve.wait_ge(xs_in, b * 16 + 16)
                    n, h = m // NH, m % NH
                    nc.vector.bn_stats(bn1[:, n, h, :], xs[:, n, h * HALF:(h + 1) * HALF]).then_inc(bn_done, 1)

            def aggregate(bn, mv, n, count, ready):
                if count is not None:
                    dve.wait_ge(bn_done, count)
                    nc.vector.memset(tick[:], 0.0)
                nc.vector.bn_aggr(mv[:, n, :], bn[:, n, :, :].rearrange("p h s -> p (h s)")).then_inc(ready, 1)

            def normalise(src, mv, rstd, ready):
                for n in range(TT):
                    nc.vector.tensor_scalar(nrm[:, n, :], src[:, n, :], mv[:, n, 0:1], rstd[:, n:n + 1],
                                            ALU.subtract, ALU.mult).then_inc(ready, 1)

            def beta2_rows():
                dve.wait_ge(beta_mm, 2)
                nc.vector.tensor_copy(beta_rows[:, 0, 0:R], bank[0:NB, 6, 0:R]).then_inc(beta_rows_ready, 1)

            def beta2_place():
                dve.wait_ge(beta_turned, 2)
                nc.vector.tensor_copy(table[:, :, BETA2:BETA2 + RB].rearrange("p b r -> p r b"),
                                      bank[:, 7, 0:RB * NB].rearrange("p (r b) -> p r b", r=RB))\
                    .then_inc(table_ready, 1)

            mod_pair(0)
            stats1(0, range(TT * NH))
            for n in range(TT):
                aggregate(bn1, mv1, n, 8 if n == 0 else None, mv1_ready)
            dve.wait_ge(rstd1_ready, 1)
            normalise(xs, mv1, rstd1, n1_ready)

            def lo(number, k, h_hi, h_lo, scale):
                dve.wait_ge(hi_ready, number + k + 1)
                nc.vector.scalar_tensor_tensor(h_lo[:, k, :], bank[:, 2 + k % 2, :], scale[:, k:k + 1],
                                               h_hi[:, k, :], ALU.mult, ALU.subtract).then_inc(lo_ready, 1)

            def iteration(b, has_y, has_prev, has_next):
                if at_start(b - 1):
                    beta2_place()
                if has_prev:
                    dve.wait_ge(rstd2_ready, b)
                    dve.wait_ge(turned, turn2(NB - 1) if isinstance(b, int) and b == NB else turn1(b) + FB)
                    normalise(xr, mv2, rstd2, n2_ready)
                for part, halves in enumerate(((0, 1, 2), (3, 4), (5, 6), (7,), ())):
                    if has_y and not has_next and part in (0, 4):
                        if part == 0:
                            dve.wait_ge(pt_out, b * 16 - 16)
                        q = 10 if part == 0 else 11
                        mod_copy(q, 4)
                        mod_place(q, 5)
                    if has_next:
                        stats1(b + 1, halves)
                    if has_next and part == 3:
                        for n in range(TT):
                            aggregate(bn1, mv1, n, b * 16 + 16 if n == 0 else None, mv1_ready)
                    if has_prev and part < 4:
                        for k in (2 * part, 2 * part + 1):
                            lo(turn2(b - 1), k, h2_hi, h2_lo, now2)
                if has_next:
                    dve.wait_ge(rstd1_ready, b + 2)
                    dve.wait_ge(turned, turn2(b - 1) + FB if has_prev else FB)
                    normalise(xs, mv1, rstd1, n1_ready)
                if at_start(b):
                    mod_copy(6, 6)
                    mod_copy(7, 7)
                    mod_place(6, 0)
                    mod_place(7, 1)
                for step in range(FB + T1_LAG):
                    k = step - BACK_LAG
                    if has_y and 0 <= k < FB:
                        n, h = k // NH, k % NH
                        dve.wait_ge(back_done, b * 8 + k + 1)
                        if k % 4 == 0:
                            dve.wait_ge(xr_in[k // 4], b * 16 + 16)
                        half = xr[:, n, h * HALF:(h + 1) * HALF]
                        nc.vector.tensor_tensor(half, bank[:, 4 + h, :], half, ALU.add).then_inc(x2_ready, 1)
                    if has_next and step >= T1_LAG:
                        lo(turn1(b + 1), step - T1_LAG, h1_hi, h1_lo, now1)
                    if has_y and 0 <= k < FB:
                        dve.wait_ge(x2_ready, b * 8 + k + 1)
                        nc.vector.bn_stats(bn2[:, n, h, :], half).then_inc(bn_done, 1)
                        if h == 1:
                            after = b * 16 + 16 if has_next else b * 16 + 8
                            aggregate(bn2, mv2, n, after + k + 1, mv2_ready)
                    if has_prev and step == FB:
                        for r in range(RB):
                            dve.wait_ge(pt_hi_ready, b * 2 - 1 + r)
                            nc.vector.scalar_tensor_tensor(pt_st[:, 1, r, :], bank[:, 6 + r, :],
                                                           now2[:, FB + r:FB + r + 1], pt_st[:, 0, r, :],
                                                           ALU.add, ALU.subtract).then_inc(pt_lo_ready, 1)
                if at_start(b):
                    mod_pair(8)
                    shift_lo(1)
                    beta2_rows()

            for k in range(FB):
                lo(0, k, h1_hi, h1_lo, now1)
                if k == 1:
                    mod_copy(2, 6)
                elif k == 3:
                    mod_copy(3, 7)
                elif k == 5:
                    mod_place(2, 4)
            mod_place(3, 5)
            shift_lo(0)
            dve.wait_ge(beta_mm, 1)
            nc.vector.tensor_copy(beta_rows, bank[0:NB, 0:NH, :]).then_inc(beta_rows_ready, 1)
            mod_pair(4)
            dve.wait_ge(beta_turned, 1)
            nc.vector.tensor_tensor(table[:, :, BETA1:BETA1 + FB].rearrange("p b t -> p t b"),
                                    bank[:, 2, 0:FB * NB].rearrange("p (t b) -> p t b", t=FB),
                                    b2_sb[:].unsqueeze(2).to_broadcast([P, FB, NB]), ALU.add).then_inc(table_ready, 1)
            iteration(0, True, False, True)
            iteration(1, True, True, True)
            with dve.Fori(2, NB - 1) as b:
                iteration(b, True, True, True)
            iteration(NB - 1, True, True, False)
            dve.wait_ge(gb_turned, 1)
            nc.vector.tensor_copy(gb_rows[:], bank[0:FB * NB, 4, 0:P]).then_inc(gb_ready, 1)
            iteration(NB, False, True, False)

            def multiply(b, q, i):
                w = width[i]
                dve.wait_ge(up_done, b * IB + i + 1)
                dve.wait_ge(silu_done, b * IB + i + 1)
                nc.vector.scalar_tensor_tensor(act[0:w, i % 2, :], bank[0:w, 2 + i % 2, :], b1_sb[0:w, i, 1:2],
                                               act[0:w, i % 2, :], ALU.add, ALU.mult).then_inc(act_done, 1)

            def act_lo_part(b, q, i):
                w = width[i]
                slot = (q * IB + i) % 4
                dve.wait_ge(act_hi_ready, b * IB + i + 1)
                nc.vector.tensor_tensor(act_lo[0:w, slot, :], act[0:w, i % 2, :], act_hi[0:w, slot, :],
                                        ALU.subtract).then_inc(act_lo_ready, 1)

            def batch(b, q, last):
                for i in range(2, IB):
                    multiply(b, q, i)
                    act_lo_part(b, q, i - 1)
                if not last:
                    multiply(b + 1, 1 - q, 0)
                act_lo_part(b, q, IB - 1)
                for r in range(RB):
                    dve.wait_ge(z_hi_ready, b * 2 + r + 1)
                    nc.vector.tensor_tensor(z_lo[:, r, :], bank[:, 4 + r, :], z_hi[:, r, :],
                                            ALU.subtract).then_inc(z_lo_ready, 1)
                if isinstance(b, int) and b == 0:
                    dve.wait_ge(b2f_in, 16)
                for m in range(TT * NH):
                    cols = slice((m % NH) * HALF, (m % NH + 1) * HALF)
                    dve.wait_ge(o_mm, b * 8 + m + 1)
                    if not at_start(b, m < 2):
                        dve.wait_ge(out_ready, b * 8 + max(m - 1, 0))
                    nc.vector.tensor_tensor(ffn[:, m % 2, :], bank[:, 6 + m % 2, :], b2f_bc[:, cols],
                                            ALU.add).then_inc(ffn_sum, 1)
                    if m == 0:
                        dve.wait_ge(gb_in, b * 16 + 16)
                    dve.wait_ge(ffn_sum, b * 8 + m + 1)
                    nc.vector.tensor_tensor(ffn[:, m % 2, :], ffn[:, m % 2, :], gb_bc[:, cols],
                                            ALU.mult).then_inc(ffn_ready, 1)
                    if m == 1 and not last:
                        multiply(b + 1, 1 - q, 1)
                        act_lo_part(b + 1, 1 - q, 0)

            multiply(0, 0, 0)
            multiply(0, 0, 1)
            act_lo_part(0, 0, 0)
            batch(0, 0, False)
            with dve.Fori(1, NB // 2) as i:
                batch(i * 2 - 1, 1, False)
                batch(i * 2, 0, False)
            batch(NB - 1, 1, True)

        @block.gpsimd
        def _(pool):
            nc.gpsimd.memset(c_pad[:], 0.0).then_inc(zero_made, 1)
            nc.gpsimd.memset(ident[:], 0.0).then_inc(zero_made, 1)
            nc.gpsimd.memset(minus_half[:], -0.5).then_inc(zero_made, 1)
            nc.gpsimd.memset(eps[:], EPS).then_inc(zero_made, 1)
            pool.wait_ge(zero_made, 4)
            nc.gpsimd.affine_select(out=ident[:], in_=ident[:], compare_op=ALU.not_equal, fill=1.0, base=0,
                                    pattern=[[-1, P]], channel_multiplier=1).then_inc(consts_made, 1)
            pool.wait_ge(off_known, 1)
            nc.gpsimd.partition_all_reduce(dense_flag[:], off_max[:], P, bass.bass_isa.ReduceOp.max)\
                .then_inc(flag_known, 1)

            def rstd(mv, ve, dst, mv_ready, count, ve_count, ready):
                pool.wait_ge(mv_ready, count)
                nc.gpsimd.tensor_tensor(ve[:], mv[:, :, 1], eps[:], ALU.add).then_inc(ve_ready, 1)
                pool.wait_ge(ve_ready, ve_count)
                nc.gpsimd.tensor_tensor(dst[:], ve[:], minus_half[:], ALU.pow).then_inc(ready, 1)

            def gate(b, t):
                if t == 0:
                    pool.wait_ge(now_ga_ready, b + 1)
                pool.wait_ge(gelu_done, b * 8 + t + 1)
                nc.gpsimd.tensor_tensor(g[:, t, :], g[:, t, :], now_ga[:, t:t + 1].to_broadcast([P, TOK]),
                                        ALU.mult).then_inc(g_ready, 1)

            rstd(mv1, ve1, rstd1, mv1_ready, 4, 1, rstd1_ready)
            pool.wait_ge(u1_in, 16)
            pool.wait_ge(attn_lo_ready, FB)
            pool.wait_ge(mod_mm, 3)
            u1_raw = xr[:, 0:2, :].rearrange("p n d -> p (n d)").rearrange("p (k r) -> p k r", k=FB)
            nc.gpsimd.tensor_copy(u1_hi[:], u1_raw).then_inc(u1_hi_ready, 1)
            pool.wait_ge(u1_hi_ready, 1)
            nc.gpsimd.tensor_tensor(u1_lo[:], u1_raw, u1_hi[:], ALU.subtract).then_inc(u1_ready, 1)

            def iteration(b, has_next):
                for t in range(5):
                    gate(b, t)
                if has_next:
                    rstd(mv1, ve1, rstd1, mv1_ready, b * 4 + 8, b * 2 + 2, rstd1_ready)
                for t in range(5, FB):
                    gate(b, t)
                rstd(mv2, ve2, rstd2, mv2_ready, b * 4 + 4, b * 2 + 3 if has_next else b * 2 + 2, rstd2_ready)

            with pool.Fori(0, NB - 1) as b:
                iteration(b, True)
            iteration(NB - 1, False)

            pool.wait_ge(y_done, FB * NB)
            pool.wait_ge(mod_mm, NCHUNK)
            done = [0]
            for m, parts in enumerate(pieces):
                if m == piece_of["u2", 0] - 1:
                    pool.wait_ge(x2_out, 32 * NB)
                    pool.wait_ge(turned, 2 * FB * NB)
                    pool.wait_ge(back_done, FB * NB)
                if m == PIECES - NH:
                    pool.wait_ge(pt_out, 16 * NB)
                pool.wait_ge(raw_in[m % 3], raw_count[m])
                for n, part in enumerate(parts):
                    src, hi_dst, lo_dst = raw_part(m % 3, part), part[5], part[6]
                    nc.gpsimd.tensor_copy(hi_dst, src).then_inc(w_hi_ready, 1)
                    done[0] += 1
                    pool.wait_ge(w_hi_ready, done[0])
                    last = nc.gpsimd.tensor_tensor(lo_dst, src, hi_dst, ALU.subtract)
                last.then_inc(w_ready, 1)

            def residual(b):
                for m in range(TT * NH):
                    n, h = m // NH, m % NH
                    half = x2t[:, n % 2, h * HALF:(h + 1) * HALF]
                    if h == 0:
                        pool.wait_ge(x2t_in[n % 2], b * 32 + 16 * (n // 2) + 16)
                    pool.wait_ge(ffn_ready, b * 8 + m + 1)
                    nc.gpsimd.tensor_tensor(half, ffn[:, m % 2, :], half, ALU.add).then_inc(out_ready, 1)

            with pool.Fori(0, NB) as b:
                residual(b)


_NAMES = ["x", "w1", "w2t", "b2", "mask", "u1", "v1", "u2", "v2", "b1_main", "b1_tail", "b2f", "ct", "wmod"]


def kernel(**inputs):
    import numpy as np
    import concourse.bacc as bacc
    from concourse.bass_utils import run_bass_kernel_spmd as run

    def get(name):
        return np.asarray(inputs["L0_" + name])

    b1 = get("ffn_b1").reshape(2, -1)
    inter = b1.shape[1]
    whole = inter // P * P
    assert whole < inter
    laid = {
        "x": get("attn_x"),
        "w1": get("attn_w1"),
        "w2t": get("attn_w2").T,
        "b2": get("attn_b2").reshape(-1, P).T,
        "mask": get("attn_sparse_mask"),
        "u1": get("ffn_U1"),
        "v1": get("ffn_V1"),
        "u2": get("ffn_U2"),
        "v2": get("ffn_V2"),
        "b1_main": b1[:, :whole].reshape(2, -1, P).transpose(2, 1, 0),
        "b1_tail": b1[:, whole:].T.reshape(inter - whole, 1, 2),
        "b2f": get("ffn_b2").reshape(1, -1),
        "ct": get("c").T,
        "wmod": get("wmod"),
    }
    nc = bacc.Bacc("TRN2", target_bir_lowering=False, num_devices=1, dynamic_dma_scratch_size=1024)
    arrays, args = {}, []
    for name in _NAMES:
        a = np.ascontiguousarray(laid[name])
        arrays[f"in_{name}"] = a
        args.append(nc.dram_tensor(f"in_{name}", a.shape, mybir.dt.from_np(a.dtype), kind="ExternalInput").ap())
    out = nc.dram_tensor("out", laid["x"].shape, F32, kind="ExternalOutput").ap()
    adaln_block(nc, *args, out)
    result = run(nc, [arrays], core_ids=[0])
    return result.results[0]["out"]
```

```python
from contextlib import ExitStack

import concourse.bass as bass
from concourse import mybir

F32 = mybir.dt.float32
F32R = mybir.dt.float32r
I32 = mybir.dt.int32
ACT = mybir.ActivationFunctionType
ALU = mybir.AluOpType
AX = mybir.AxisListType

P = 128
EPS = 1e-5
GATE_FLOOR = 0.25


def adaln_block(nc, x, w1, w2t, b2, mask, u1, v1, u2, v2, b1_main, b1_tail, b2f, ct, wmod, out):
    NB, TOK, D = x.shape
    FB = D // P
    TT = TOK // P
    R = u1.shape[1]
    RB = R // P
    INTER = u2.shape[0]
    IB = -(-INTER // P)
    HALF = 512
    NH = D // HALF
    width = [min(P, INTER - P * i) for i in range(IB)]
    assert width[-1] == P // 2 and TOK == HALF and IB % 2 == 0 and NB % 2 == 0 and RB == 2

    def band_cols(s):
        return max(0, P * (s - 1)), min(D, P * (s + 2))

    off_band = []
    for s in range(FB):
        lo_c, hi_c = band_cols(s)
        for a, e in ((0, lo_c), (hi_c, D)):
            while a < e:
                off_band.append((s, a, min(a + HALF, e)))
                a = min(a + HALF, e)

    SCALE1, BETA1, GA, SCALE2, BETA2 = 0, FB, 2 * FB, 3 * FB, 4 * FB
    NCOL = 4 * FB + RB

    x_tiles = x.rearrange("b (n p) d -> b p n d", p=P)
    out_tiles = out.rearrange("b (n p) d -> b n p d", p=P)
    x2_dram = nc.dram_tensor("x2_dram", [NB, TOK, D], F32, kind="Internal").ap()
    x2_store = x2_dram.rearrange("b (n p) d -> b p n d", p=P)
    x2_tiles = x2_dram.rearrange("b (n p) d -> b n p d", p=P)
    pt_dram = nc.dram_tensor("pt_dram", [NB, P, 2, RB, TOK], F32, kind="Internal").ap()
    gb_dram = nc.dram_tensor("gb_dram", [NB, 1, D], F32, kind="Internal").ap()

    with ExitStack() as ctx:
        def sem(name):
            return ctx.enter_context(nc.semaphore(name))

        def buf(scope, name, shape, dt=F32):
            return scope.enter_context(nc.sbuf_tensor(name, shape, dt))

        bank = ctx.enter_context(nc.psum_tensor("bank", [P, 8, HALF], F32))

        b1_sb = buf(ctx, "b1_sb", [P, IB, 2])
        p01 = ctx.enter_context(ExitStack())
        attn_hi = buf(p01, "attn_hi", [P, FB, D], F32R)
        with ExitStack() as staging:
            masked = buf(staging, "masked", [P, FB, D])
        off_junk = masked[:, 0, 0:HALF]
        attn_lo = buf(p01, "attn_lo", [P, FB, D], F32R)
        sh = buf(p01, "sh", [P, 2, FB, NB])
        sh_hi = buf(p01, "sh_hi", [P, 2, FB, NB], F32R)
        sh_lo = buf(p01, "sh_lo", [P, 2, FB, NB], F32R)
        with ExitStack() as p0:
            w1_sb = buf(p0, "w1_sb", [P, FB, D])
            w2t_sb = buf(p0, "w2t_sb", [P, FB, D])
            mask_sb = buf(p0, "mask_sb", [P, FB, D])
            wm_sb = buf(p0, "wm_sb", [P, 2, FB, HALF])
            x0 = buf(p0, "x0", [P, TT, D])
        with ExitStack() as p1:
            xs = buf(p1, "xs", [P, TT, D])
            h1_hi = buf(p1, "h1_hi", [P, FB, TOK], F32R)
            h1_lo = buf(p1, "h1_lo", [P, FB, TOK], F32R)
            xr = buf(p1, "xr", [P, TT, D])
            nrm = buf(p1, "nrm", [P, TT, D])
            g = buf(p1, "g", [P, FB, TOK])
            h2_hi = buf(p1, "h2_hi", [P, FB, TOK], F32R)
            h2_lo = buf(p1, "h2_lo", [P, FB, TOK], F32R)
            u1_hi = buf(p1, "u1_hi", [P, FB, R], F32R)
            u1_lo = buf(p1, "u1_lo", [P, FB, R], F32R)
            pt_st = buf(p1, "pt_st", [P, 2, RB, TOK], F32R)
            beta_rows = pt_st[0:NB, 1].bitcast(F32)
            mod_rows = pt_st[:, 0].bitcast(F32)
            ident = buf(p1, "ident", [P, P])
            table = buf(p1, "table", [P, NB, NCOL])
            b2_sb = buf(p1, "b2_sb", [P, FB])
            minus_half = buf(p1, "minus_half", [P, TT])
            tick = buf(p1, "tick", [P, 1])
            off_any = buf(p1, "off_any", [P, len(off_band)])
            off_max = buf(p1, "off_max", [P, 1])
            dense_flag = buf(p1, "dense_flag", [P, 1])
            c_sb = buf(p1, "c_sb", [P, FB, NB])
            c_pad = buf(p1, "c_pad", [P, FB, 32])
            mod_sum = buf(p1, "mod_sum", [P, 4, NB])
            gate_sign = buf(p1, "gate_sign", [P, 4, NB])
            gate_size = buf(p1, "gate_size", [P, 4, NB])
            gate_big = buf(p1, "gate_big", [P, 4, NB])
            gb_feat = buf(p1, "gb_feat", [P, FB, NB])
            gb_rows = buf(p1, "gb_rows", [FB * NB, P])
            bn1 = buf(p1, "bn1", [P, TT, 2, 6])
            bn2 = buf(p1, "bn2", [P, TT, 2, 6])
            mv1 = buf(p1, "mv1", [P, TT, 2])
            mv2 = buf(p1, "mv2", [P, TT, 2])
            ve1 = buf(p1, "ve1", [P, TT])
            ve2 = buf(p1, "ve2", [P, TT])
            rstd1 = buf(p1, "rstd1", [P, TT])
            rstd2 = buf(p1, "rstd2", [P, TT])
            now1 = buf(p1, "now1", [P, FB])
            now_beta = buf(p1, "now_beta", [P, FB])
            now_ga = buf(p1, "now_ga", [P, FB])
            now2 = buf(p1, "now2", [P, FB + RB])
            eps = buf(p1, "eps", [P, TT])
        p01.close()
        p2 = ctx
        v1_hi = buf(p2, "v1_hi", [P, RB, 2 * INTER], F32R)
        v1_lo = buf(p2, "v1_lo", [P, RB, 2 * INTER], F32R)
        with ExitStack() as p2a:
            raw = buf(p2a, "raw", [P, 3, RB * HALF])
        x2t = buf(p2, "x2t", [P, TT, D])
        pt = buf(p2, "pt", [P, 2, 2, RB, TOK], F32R)
        u2_hi = buf(p2, "u2_hi", [P, IB, R], F32R)
        u2_lo = buf(p2, "u2_lo", [P, IB, R], F32R)
        v2_hi = buf(p2, "v2_hi", [P, RB, D], F32R)
        v2_lo = buf(p2, "v2_lo", [P, RB, D], F32R)
        act = buf(p2, "act", [P, 2, TOK])
        act_hi = buf(p2, "act_hi", [P, 4, TOK], F32R)
        act_lo = buf(p2, "act_lo", [P, 4, TOK], F32R)
        z_hi = buf(p2, "z_hi", [P, RB, TOK], F32R)
        z_lo = buf(p2, "z_lo", [P, RB, TOK], F32R)
        ffn = buf(p2, "ffn", [P, 3, HALF])
        gb_bc = buf(p2, "gb_bc", [P, D])
        b2f_bc = buf(p2, "b2f_bc", [P, D])

        const_in = sem("const_in")
        w_in = [sem(f"w_in{k}") for k in range(FB)]
        mask_in = [sem("mask_in0"), sem("mask_in1")]
        wm_in = [sem(f"wm_in{i}") for i in range(3)]
        consts_made = sem("consts_made")
        zero_made = sem("zero_made")
        c_ready = sem("c_ready")
        dve_step = sem("dve_step")
        off_known = sem("off_known")
        flag_known = sem("flag_known")
        attn_mm = sem("attn_mm")
        masked_ready = sem("masked_ready")
        attn_hi_ready = sem("attn_hi_ready")
        attn_lo_ready = sem("attn_lo_ready")
        dn_mm = sem("dn_mm")
        dn_masked = sem("dn_masked")
        dn_hi = sem("dn_hi")
        dn_lo = sem("dn_lo")
        mod_mm = sem("mod_mm")
        mod_rows_ready = sem("mod_rows_ready")
        mod_turned = sem("mod_turned")
        mod_read = sem("mod_read")
        mod_placed = sem("mod_placed")
        sh_hi_ready = sem("sh_hi_ready")
        sh_lo_ready = sem("sh_lo_ready")
        gb_turned = sem("gb_turned")
        gb_ready = sem("gb_ready")
        gb_out = sem("gb_out")
        beta_mm = sem("beta_mm")
        beta_rows_ready = sem("beta_rows_ready")
        beta_turned = sem("beta_turned")
        table_ready = sem("table_ready")
        u1_in = sem("u1_in")
        u1_hi_ready = sem("u1_hi_ready")
        u1_ready = sem("u1_ready")
        xs_in = sem("xs_in")
        x0_in = sem("x0_in")
        xr_in = [sem("xr_in0"), sem("xr_in1")]
        x2_out = sem("x2_out")
        bn_done = sem("bn_done")
        mv1_ready = sem("mv1_ready")
        mv2_ready = sem("mv2_ready")
        ve_ready = sem("ve_ready")
        rstd1_ready = sem("rstd1_ready")
        rstd2_ready = sem("rstd2_ready")
        n1_ready = sem("n1_ready")
        n2_ready = sem("n2_ready")
        turned = sem("turned")
        hi_ready = sem("hi_ready")
        lo_ready = sem("lo_ready")
        now1_ready = sem("now1_ready")
        now_beta_ready = sem("now_beta_ready")
        now_ga_ready = sem("now_ga_ready")
        now2_ready = sem("now2_ready")
        now_beta2_ready = sem("now_beta2_ready")
        y_done = sem("y_done")
        gelu_done = sem("gelu_done")
        g_ready = sem("g_ready")
        back_done = sem("back_done")
        x2_ready = sem("x2_ready")
        p_done = sem("p_done")
        pt_hi_ready = sem("pt_hi_ready")
        pt_lo_ready = sem("pt_lo_ready")
        pt_out = sem("pt_out")
        raw_in = [sem(f"raw_in{i}") for i in range(3)]
        w_hi_ready = sem("w_hi_ready")
        w_ready = sem("w_ready")
        pt_in = [sem("pt_in0"), sem("pt_in1")]
        gate_done = sem("gate_done")
        up_done = sem("up_done")
        silu_done = sem("silu_done")
        act_done = sem("act_done")
        act_hi_ready = sem("act_hi_ready")
        act_lo_ready = sem("act_lo_ready")
        z_step = sem("z_step")
        z_hi_ready = sem("z_hi_ready")
        z_lo_ready = sem("z_lo_ready")
        o_mm = sem("o_mm")
        ffn_sum = sem("ffn_sum")
        ffn_ready = sem("ffn_ready")
        out_ready = sem("out_ready")
        b2f_in = sem("b2f_in")
        gb_in = sem("gb_in")
        x2t_in = [sem(f"x2t_in{n}") for n in range(TT)]
        out_stored = sem("out_stored")

        NCHUNK = wmod.shape[1] // HALF
        wm_view = wmod.rearrange("(k p) n -> p k n", p=P)
        SA, CA, GA_KIND, SB, CB, GB_KIND = range(6)
        KINDS = [CA, SA, GA_KIND, CB, SB, GB_KIND]
        WM_PLACE = [0, 1] * (NCHUNK // 2 - 1) + [2, 2]

        def chunk_cols(q):
            return slice(KINDS[q // 2] * D + q % 2 * HALF, KINDS[q // 2] * D + (q % 2 + 1) * HALF)

        late_chunk = xs[:].rearrange("p n d -> p (n d)").rearrange("p (k c) -> p k c", k=FB)

        def wm_chunk(q):
            return late_chunk if WM_PLACE[q] == 2 else wm_sb[:, WM_PLACE[q]]

        def before(q):
            return [c for c in range(q) if WM_PLACE[c] == WM_PLACE[q]]

        BACK_LAG, T1_LAG = 1, 2

        def at_start(b, early=True):
            return isinstance(b, int) and b == 0 and early

        def turn1(b):
            return 0 if isinstance(b, int) and b == 0 else b * 16 - 8

        def turn2(b):
            return b * 16 + (8 if isinstance(b, int) and b == NB - 1 else 16)

        UP = INTER + width[-1]
        GROUPS = [(a, min(a + HALF, INTER)) for a in range(0, INTER, HALF)]
        v1_view = v1.rearrange("(k p) f -> p k f", p=P)
        v2_view = v2.rearrange("(k p) f -> p k f", p=P)
        pieces = []
        piece_of = {}
        for q, (a, e) in enumerate(GROUPS):
            for name, base, at in (("gate", 0, 0), ("up", INTER, UP)):
                whole = (e - a) // P * P
                spans = [(a, e, a)] if name == "gate" or whole == e - a else \
                    [(a, a + whole, a), (a + whole, e, INTER - UP)]
                pieces.append([(v1_view[:, :, base + f:base + l], P, RB, l - f, RB * (f - a),
                                v1_hi[:, :, at + to:at + to + l - f], v1_lo[:, :, at + to:at + to + l - f])
                               for f, l, to in spans])
                piece_of[name, q] = len(pieces)
            full, rest = (e - a) // P, (e - a) % P
            i0 = a // P
            parts = [(u2[a:a + full * P, :].rearrange("(i p) r -> p i r", p=P), P, full, R, 0,
                      u2_hi[:, i0:i0 + full, :], u2_lo[:, i0:i0 + full, :])]
            if rest:
                parts.append((u2[a + full * P:e, :].rearrange("(i p) r -> p i r", i=1), rest, 1, R, full * R,
                              u2_hi[0:rest, i0 + full:i0 + full + 1, :],
                              u2_lo[0:rest, i0 + full:i0 + full + 1, :]))
            pieces.append(parts)
            piece_of["u2", q] = len(pieces)
        for h in range(NH):
            pieces.append([(v2_view[:, :, h * HALF:(h + 1) * HALF], P, RB, HALF, 0,
                            v2_hi[:, :, h * HALF:(h + 1) * HALF], v2_lo[:, :, h * HALF:(h + 1) * HALF])])
        PIECES = len(pieces)

        def raw_part(slot, part):
            _, rows, blocks, n, off, _, _ = part
            return raw[0:rows, slot, off:off + blocks * n].rearrange("p (k n) -> p k n", k=blocks)

        raw_count = []
        seen = [0, 0, 0]
        for m, parts in enumerate(pieces):
            seen[m % 3] += 16 * len(parts)
            raw_count.append(seen[m % 3])

        BAND_ORDER = [6, 7] + list(range(6))

        block = ctx.enter_context(nc.Block())

        @block.sync
        def _(sp):
            sp.dma_start(c_sb[:], ct.rearrange("(k p) b -> p k b", p=P)).then_inc(const_in, 16)
            sp.dma_start(b2_sb[:], b2[:, :]).then_inc(const_in, 16)
            sp.dma_start(b1_sb[:, 0:IB - 1, :], b1_main[:, :, :]).then_inc(const_in, 16)
            sp.dma_start(b1_sb[0:width[-1], IB - 1:IB, :], b1_tail[:, :, :]).then_inc(const_in, 16)
            for k in range(FB):
                rows = slice(k * P, (k + 1) * P)
                sp.dma_start(w1_sb[:, k, :], w1[rows, :]).then_inc(w_in[k], 16)
                sp.dma_start(w2t_sb[:, k, :], w2t[rows, :]).then_inc(w_in[k], 16)
            sp.dma_start(x0[:], x_tiles[0]).then_inc(x0_in, 16)
            for half in range(2):
                k = slice(half * FB // 2, (half + 1) * FB // 2)
                sp.dma_start(mask_sb[:, k, :], mask.rearrange("(k p) t -> p k t", p=P)[:, k, :])\
                    .then_inc(mask_in[half], 16)

            def wm_load(q):
                if before(q):
                    sp.wait_ge(mod_mm, before(q)[-1] + 1)
                sp.dma_start(wm_chunk(q), wm_view[:, :, chunk_cols(q)]).then_inc(wm_in[WM_PLACE[q]], 16)

            for q in range(2):
                wm_load(q)
            for q in range(2, 4):
                wm_load(q)
            u1_raw = xr[:, 0:2, :].rearrange("p n d -> p (n d)").rearrange("p (k r) -> p k r", k=FB)
            sp.dma_start(u1_raw, u1.rearrange("(k p) r -> p k r", p=P)).then_inc(u1_in, 16)
            for q in range(4, 6):
                wm_load(q)
            sp.dma_start(xs[:], x_tiles[1]).then_inc(xs_in, 16)

            def raw_load(m):
                if m >= 3:
                    sp.wait_ge(w_ready, m - 2)
                for part in pieces[m]:
                    sp.dma_start(raw_part(m % 3, part), part[0]).then_inc(raw_in[m % 3], 16)

            def iteration(b, has_y, has_prev, has_load, chunks=(), weights=False):
                if weights:
                    wm_load(NCHUNK - 1)
                if has_y:
                    if has_prev:
                        sp.wait_ge(x2_out, b * 32)
                    else:
                        sp.wait_ge(u1_ready, 1)
                    for half in range(2):
                        n = slice(half * TT // 2, (half + 1) * TT // 2)
                        sp.dma_start(xr[:, n, :], x_tiles[b, :, n, :]).then_inc(xr_in[half], 16)
                for q in chunks:
                    if q == NCHUNK - 2:
                        sp.wait_ge(n1_ready, NB * 4)
                    wm_load(q)
                if has_load:
                    sp.wait_ge(n1_ready, b * 4 + 8)
                    sp.dma_start(xs[:], x_tiles[b + 2]).then_inc(xs_in, 16)
                if weights:
                    sp.wait_ge(y_done, FB * NB)
                    sp.dma_start(pt[:, 0].bitcast(F32), pt_dram[0]).then_inc(pt_in[0], 16)
                    for m in range(3):
                        raw_load(m)
                if has_y:
                    sp.wait_ge(x2_ready, b * 8 + 4)
                    sp.dma_start(x2_store[b, :, 0:TT // 2, :], xr[:, 0:TT // 2, :]).then_inc(x2_out, 16)
                if has_prev:
                    sp.wait_ge(pt_lo_ready, b * 2)
                    sp.dma_start(pt_dram[b - 1], pt_st[:].bitcast(F32)).then_inc(pt_out, 16)
                if has_y:
                    sp.wait_ge(n2_ready, b * 4 + 4)
                    sp.dma_start(x2_store[b, :, TT // 2:TT, :], xr[:, TT // 2:TT, :]).then_inc(x2_out, 16)

            iteration(0, True, False, True, (6, 7, 8, 9))
            with sp.Fori(1, NB - 2) as b:
                iteration(b, True, True, True)
            iteration(NB - 2, True, True, False, (10,))
            iteration(NB - 1, True, True, False, (), True)
            for m in range(3, 7):
                raw_load(m)
                if m == 4:
                    sp.wait_ge(x2_out, 32 * NB)
                    sp.dma_start(pt[:, 1].bitcast(F32), pt_dram[1]).then_inc(pt_in[1], 16)
            sp.wait_ge(pt_lo_ready, 2 * NB)
            sp.dma_start(pt_dram[NB - 1], pt_st[:].bitcast(F32)).then_inc(pt_out, 16)
            sp.wait_ge(gb_ready, 1)
            for k in range(FB):
                sp.dma_start(gb_dram[:, 0, k * P:(k + 1) * P], gb_rows[k * NB:(k + 1) * NB, :]).then_inc(gb_out, 16)

            for m in range(7, PIECES):
                raw_load(m)
            sp.wait_ge(pt_out, 16 * NB)
            sp.wait_ge(gb_out, 16 * FB)
            sp.dma_start(b2f_bc[:], b2f[:, :].broadcast_to([P, D])).then_inc(b2f_in, 16)
            sp.wait_ge(w_ready, PIECES)

            def tile_in(b, n):
                sp.dma_start(x2t[:, n, :], x2_tiles[b, n]).then_inc(x2t_in[n], 16)

            def batch(b, q, last):
                if not last and not at_start(b):
                    sp.wait_ge(gate_done, b * IB)
                    sp.dma_start(pt[:, 1 - q].bitcast(F32), pt_dram[b + 1]).then_inc(pt_in[1 - q], 16)
                if not at_start(b):
                    sp.wait_ge(ffn_ready, b * 8)
                sp.dma_start(gb_bc[:], gb_dram[b].broadcast_to([P, D])).then_inc(gb_in, 16)
                for n in range(TT):
                    sp.wait_ge(out_ready, b * 8 + 2 * n + 2)
                    sp.dma_start(out_tiles[b, n], x2t[:, n, :]).then_inc(out_stored, 16)
                    if not last:
                        sp.wait_ge(out_stored, b * 64 + 16 * n + 16)
                        tile_in(b + 1, n)

            for n in range(TT):
                tile_in(0, n)
            batch(0, 0, False)
            with sp.Fori(1, NB // 2) as i:
                batch(i * 2 - 1, 1, False)
                batch(i * 2, 0, False)
            batch(NB - 1, 1, True)
            sp.wait_ge(out_stored, 64 * NB)

        @block.tensor
        def _(pe):
            def three(acc, s_hi, s_lo, m_hi, m_lo, start, stop):
                nc.tensor.matmul(acc, s_hi, m_hi, start=start, stop=False)
                nc.tensor.matmul(acc, s_hi, m_lo, start=False, stop=False)
                return nc.tensor.matmul(acc, s_lo, m_hi, start=False, stop=stop)

            def attn_product(acc, s, a, e):
                for k in range(FB):
                    last = nc.tensor.matmul(acc, w1_sb[:, k, s * P:(s + 1) * P], w2t_sb[:, k, a:e],
                                            start=(k == 0), stop=(k == FB - 1))
                return last

            for k in range(FB):
                pe.wait_ge(w_in[k], 32)
                for s in BAND_ORDER:
                    a, e = band_cols(s)
                    last = nc.tensor.matmul(bank[:, s, 0:e - a], w1_sb[:, k, s * P:(s + 1) * P], w2t_sb[:, k, a:e],
                                            start=(k == 0), stop=(k == FB - 1))
                    if k == FB - 1:
                        last.then_inc(attn_mm, 1)
            pe.wait_ge(flag_known, 1)
            dense = nc.tensor.value_load(dense_flag[0:1, 0:1].bitcast(I32))
            with nc.tensor.If(dense != 0):
                pe.wait_ge(masked_ready, FB)
                for n, (s, a, e) in enumerate(off_band):
                    if n >= 2:
                        pe.wait_ge(dn_masked, n - 1)
                    attn_product(bank[:, n % 2, 0:e - a], s, a, e).then_inc(dn_mm, 1)

            def mod_product(q, rows_bank):
                pe.wait_ge(wm_in[WM_PLACE[q]], 16 * len(before(q)) + 16)
                if q >= 2:
                    pe.wait_ge(mod_rows_ready, q - 1)
                for k in range(FB):
                    j = k % 4
                    last = nc.tensor.matmul(bank[32 * j:32 * j + 32, rows_bank, :], c_pad[:, k, :],
                                            wm_chunk(q)[:, k, :], start=(k < 4), stop=(k >= 4),
                                            skip_group_check=True)
                last.then_inc(mod_mm, 1)

            def mod_turn(q, turn_bank):
                pe.wait_ge(mod_rows_ready, q + 1)
                if q >= 2:
                    pe.wait_ge(mod_read, q - 1)
                for j in range(4):
                    cols = slice(j * P, (j + 1) * P)
                    last = nc.tensor.transpose(bank[:, turn_bank, cols], mod_rows[:, q % 2, cols], ident[:])
                last.then_inc(mod_turned, 1)

            def mod_pair(q):
                mod_product(q, 6)
                mod_product(q + 1, 7)
                mod_turn(q, 4)
                mod_turn(q + 1, 5)

            pe.wait_ge(consts_made, 1)
            pe.wait_ge(c_ready, 1)
            pe.wait_ge(masked_ready, 2)
            mod_product(0, 6)
            mod_product(1, 7)
            pe.wait_ge(masked_ready, FB)
            mod_turn(0, 4)
            mod_turn(1, 5)

            def turn(number, k, src=nrm):
                if not (isinstance(number, int) and number < 2):
                    pe.wait_ge(lo_ready, number - 1)
                for n in range(TT):
                    last = nc.tensor.transpose(bank[:, 2 + k % 2, n * P:(n + 1) * P],
                                               src[:, n, k * P:(k + 1) * P], ident[:])
                last.then_inc(turned, 1)

            pe.wait_ge(n1_ready, 4)
            for k in range(FB):
                turn(k, k, x0)
                if k == 3:
                    mod_product(2, 6)
                elif k == 5:
                    mod_turn(2, 4)
            mod_product(3, 7)
            mod_turn(3, 5)

            def shift_product(v, acc, w_hi, w_lo, s, start, stop):
                nc.tensor.matmul(acc, sh_hi[:, v, s, :], w_hi, start=start, stop=False, skip_group_check=True)
                nc.tensor.matmul(acc, sh_hi[:, v, s, :], w_lo, start=False, stop=False, skip_group_check=True)
                return nc.tensor.matmul(acc, sh_lo[:, v, s, :], w_hi, start=False, stop=stop, skip_group_check=True)

            def attn_shift(s, a, e, start, stop):
                h = a // HALF
                return shift_product(0, bank[0:NB, 4 + h, a - h * HALF:e - h * HALF], attn_hi[:, s, a:e],
                                     attn_lo[:, s, a:e], s, start, stop)

            def by_bank(parts):
                return [(s, max(a, h * HALF), min(e, (h + 1) * HALF)) for h in range(NH) for s, a, e in parts
                        if max(a, h * HALF) < min(e, (h + 1) * HALF)]

            pe.wait_ge(sh_lo_ready, 1)
            pe.wait_ge(attn_lo_ready, FB)
            near = by_bank([(s, *band_cols(s)) for s in range(FB)])
            for h in range(NH):
                of_bank = [part for part in near if part[1] // HALF == h]
                for part in of_bank[:-1]:
                    attn_shift(*part, part == of_bank[0], False)
            with nc.tensor.If(dense != 0):
                pe.wait_ge(dn_lo, len(off_band))
                for part in by_bank(off_band):
                    attn_shift(*part, False, False)
            for h in range(NH):
                part = [part for part in near if part[1] // HALF == h][-1]
                last = attn_shift(*part, False, True)
            last.then_inc(beta_mm, 1)

            def beta2_product():
                pe.wait_ge(sh_lo_ready, 2)
                pe.wait_ge(u1_ready, 1)
                for k in range(FB):
                    last = shift_product(1, bank[0:NB, 6, 0:R], u1_hi[:, k, :], u1_lo[:, k, :], k,
                                         k == 0, k == FB - 1)
                last.then_inc(beta_mm, 1)

            def beta_turn(v, turn_bank, blocks):
                pe.wait_ge(beta_rows_ready, v + 1)
                for t in range(blocks):
                    last = nc.tensor.transpose(bank[:, turn_bank, t * NB:(t + 1) * NB],
                                               beta_rows[:, t // 4, t % 4 * P:(t % 4 + 1) * P], ident[0:NB, 0:NB])
                last.then_inc(beta_turned, 1)

            def y(b, t):
                first = turn1(b)
                if not at_start(b, t < 2):
                    pe.wait_ge(gelu_done, b * 8 + t - 1)
                pe.wait_ge(lo_ready, first + min(t + 2, FB))
                near = [s for s in range(FB) if abs(s - t) <= 1]
                far = [s for s in range(FB) if abs(s - t) > 1]
                acc = bank[:, t % 2, :]
                cols = slice(t * P, (t + 1) * P)
                for s in near[:-1]:
                    three(acc, attn_hi[:, s, cols], attn_lo[:, s, cols], h1_hi[:, s, :], h1_lo[:, s, :],
                          s == near[0], False)
                with nc.tensor.If(dense != 0):
                    pe.wait_ge(lo_ready, first + FB)
                    for s in far:
                        three(acc, attn_hi[:, s, cols], attn_lo[:, s, cols], h1_hi[:, s, :], h1_lo[:, s, :],
                              False, False)
                s = near[-1]
                three(acc, attn_hi[:, s, cols], attn_lo[:, s, cols], h1_hi[:, s, :], h1_lo[:, s, :],
                      False, True).then_inc(y_done, 1)

            def turn_back(b, k):
                if not at_start(b, k < 2):
                    pe.wait_ge(x2_ready, b * 8 + k - 1)
                if k == 0:
                    pe.wait_ge(g_ready, b * 8 + 8)
                    if at_start(b):
                        pe.wait_ge(mod_read, 6)
                n = k // 2
                for j in range(4):
                    last = nc.tensor.transpose(bank[:, 4 + k % 2, j * P:(j + 1) * P],
                                               g[:, 4 * (k % 2) + j, n * P:(n + 1) * P], ident[:])
                last.then_inc(back_done, 1)

            def p_product(b, k):
                pe.wait_ge(lo_ready, turn2(b) + k + 1)
                if k == 0 and not at_start(b):
                    pe.wait_ge(pt_lo_ready, b * 2)
                for r in range(RB):
                    cols = slice(r * P, (r + 1) * P)
                    last = three(bank[:, 6 + r, :], u1_hi[:, k, cols], u1_lo[:, k, cols],
                                 h2_hi[:, k, :], h2_lo[:, k, :], k == 0, k == FB - 1)
                if k == FB - 1:
                    last.then_inc(p_done, 1)

            def iteration(b, has_y, has_prev, has_next):
                for t in range(FB):
                    if has_y:
                        y(b, t)
                    if at_start(b, t == 0):
                        beta_turn(0, 2, FB)
                    if at_start(b, t == 2):
                        mod_pair(4)
                    if at_start(b - 1, t in (2, 3)):
                        mod_product(6 + t, 4 + t)
                    if has_y and not has_next:
                        if t == 1:
                            pe.wait_ge(x2_ready, b * 8)
                            mod_product(10, 4)
                        elif t == 2:
                            mod_turn(10, 5)
                    if has_prev and 3 <= t <= 6:
                        if t == 3:
                            pe.wait_ge(n2_ready, b * 4)
                        for k in (2 * (t - 3), 2 * (t - 3) + 1):
                            turn(turn2(b - 1) + k, k)
                    if at_start(b - 1, t == 3):
                        pe.wait_ge(x2_ready, FB)
                        mod_turn(8, 4)
                        mod_turn(9, 5)
                    elif at_start(b - 1, t == 5):
                        pe.wait_ge(mod_placed, 10)
                        beta2_product()
                    elif at_start(b - 1, t == 6):
                        beta_turn(1, 7, RB)
                    if has_y and not has_next:
                        if t == FB - 2:
                            mod_product(11, 4)
                        elif t == FB - 1:
                            mod_turn(11, 5)
                            pe.wait_ge(mod_read, NCHUNK)
                for step in range(FB + T1_LAG):
                    if has_y and not has_next and step < FB:
                        turn_back(b, step)
                    if has_prev and step < FB:
                        if at_start(b - 1, step == 0):
                            pe.wait_ge(table_ready, 2)
                        if step < FB - 1 or not has_next:
                            p_product(b - 1, step)
                    if has_next and BACK_LAG <= step < FB + BACK_LAG:
                        turn_back(b, step - BACK_LAG)
                    if has_next and step >= T1_LAG:
                        k = step - T1_LAG
                        if k == 0:
                            pe.wait_ge(n1_ready, b * 4 + 8)
                        turn(turn1(b + 1) + k, k)
                    if has_prev and has_next and step == FB:
                        p_product(b - 1, FB - 1)
                    if at_start(b, step == 4):
                        mod_product(6, 6)
                    elif at_start(b, step == 6):
                        mod_product(7, 7)
                        pe.wait_ge(gelu_done, FB)
                        mod_turn(6, 0)
                    elif at_start(b, step == 8):
                        mod_turn(7, 1)
                if at_start(b):
                    pe.wait_ge(mod_read, 8)

            iteration(0, True, False, True)
            iteration(1, True, True, True)
            with pe.Fori(2, NB - 1) as b:
                iteration(b, True, True, True)
            iteration(NB - 1, True, True, False)

            def h_waits(b, q, i):
                if i == 0:
                    pe.wait_ge(pt_in[q], (b - q) * 8 + 16)
                if not at_start(b, i < 2):
                    pe.wait_ge(act_done, b * IB + i - 1)

            def h_part(q, i, acc, name, v_hi, v_lo):
                if i % 4 == 0 or i == IB - 1:
                    pe.wait_ge(w_ready, piece_of[name, i // 4])
                for r in range(RB):
                    last = three(acc, v_hi[:, r], v_lo[:, r], pt[:, q, 0, r, :], pt[:, q, 1, r, :],
                                 r == 0, r == RB - 1)
                return last

            def gate_product(b, q, i):
                cols = slice(i * P, i * P + P)
                h_waits(b, q, i)
                h_part(q, i, bank[:, i % 2, :], "gate", v1_hi[:, :, cols], v1_lo[:, :, cols]).then_inc(gate_done, 1)

            def up_product(b, q, i):
                cols = slice(UP + i * P, UP + i * P + P)
                h_part(q, i, bank[:, 2 + i % 2, :], "up", v1_hi[:, :, cols], v1_lo[:, :, cols]).then_inc(up_done, 1)

            def h_product(b, q, i):
                if i < IB - 1:
                    gate_product(b, q, i)
                    up_product(b, q, i)
                else:
                    h_waits(b, q, i)
                    cols = slice(i * P, i * P + P)
                    h_part(q, i, bank[:, i % 2, :], "up", v1_hi[:, :, cols], v1_lo[:, :, cols]).then_inc(gate_done, 1)

            def z_product(b, q, i):
                pe.wait_ge(act_lo_ready, b * IB + i + 1)
                if i % 4 == 0:
                    pe.wait_ge(w_ready, piece_of["u2", i // 4])
                if at_start(b, i == 0):
                    pe.wait_ge(gb_ready, 1)
                elif i == 0:
                    pe.wait_ge(z_lo_ready, b * 2)
                w = width[i]
                slot = (q * IB + i) % 4
                for r in range(RB):
                    cols = slice(r * P, (r + 1) * P)
                    last = three(bank[:, 4 + r, :], u2_hi[0:w, i, cols], u2_lo[0:w, i, cols],
                                 act_hi[0:w, slot, :], act_lo[0:w, slot, :], i == 0, i == IB - 1)
                last.then_inc(z_step, 1)

            def out_product(b):
                pe.wait_ge(z_lo_ready, b * 2 + 2)
                pe.wait_ge(w_ready, PIECES)
                if at_start(b):
                    pe.wait_ge(pt_lo_ready, 2 * NB)
                for m in range(TT * NH):
                    n, h = m // NH, m % NH
                    if not at_start(b, m < 2):
                        pe.wait_ge(ffn_sum, b * 8 + max(m - 1, 0))
                    toks, cols = slice(n * P, (n + 1) * P), slice(h * HALF, (h + 1) * HALF)
                    for r in range(RB):
                        last = three(bank[:, 6 + m % 2, :], z_hi[:, r, toks], z_lo[:, r, toks],
                                     v2_hi[:, r, cols], v2_lo[:, r, cols], r == 0, r == RB - 1)
                    last.then_inc(o_mm, 1)

            def batch(b, q, last):
                for i in range(2, IB):
                    h_product(b, q, i)
                    z_product(b, q, i - 2)
                if not last:
                    gate_product(b + 1, 1 - q, 0)
                z_product(b, q, IB - 2)
                z_product(b, q, IB - 1)
                if not last:
                    up_product(b + 1, 1 - q, 0)
                    h_product(b + 1, 1 - q, 1)
                out_product(b)

            pe.wait_ge(x2_ready, FB * NB)
            pe.wait_ge(mod_placed, NCHUNK)
            nc.tensor.transpose(bank[0:FB * NB, 4, 0:P], gb_feat[:].rearrange("p k b -> p (k b)"),
                                ident[:]).then_inc(gb_turned, 1)
            for i in range(2):
                pe.wait_ge(gelu_done, 8 * NB)
                gate_product(0, 0, i)
            pe.wait_ge(n2_ready, NB * 4)
            for k in range(FB + 2):
                if k < FB:
                    turn(turn2(NB - 1) + k, k)
                if k >= 2:
                    p_product(NB - 1, k - 2)

            for i in range(2):
                pe.wait_ge(lo_ready, turn2(NB - 1) + FB)
                up_product(0, 0, i)
            batch(0, 0, False)
            with pe.Fori(1, NB // 2) as i:
                batch(i * 2 - 1, 1, False)
                batch(i * 2, 0, False)
            batch(NB - 1, 1, True)

        @block.scalar
        def _(ae):
            ae.wait_ge(const_in, 64)
            ae.wait_ge(zero_made, 1)
            nc.scalar.activation(c_pad[:, :, 0:NB], c_sb[:], ACT.Silu).then_inc(c_ready, 1)
            for n, s in enumerate(BAND_ORDER):
                a, e = band_cols(s)
                ae.wait_ge(masked_ready, n + 1)
                nc.scalar.activation(attn_hi[:, s, a:e], masked[:, s, a:e],
                                     ACT.Copy).then_inc(attn_hi_ready, 1)
            ae.wait_ge(flag_known, 1)
            dense = nc.scalar.value_load(dense_flag[0:1, 0:1].bitcast(I32))
            with nc.scalar.If(dense != 0):
                for n, (s, a, e) in enumerate(off_band):
                    ae.wait_ge(dn_masked, n + 1)
                    nc.scalar.activation(attn_hi[:, s, a:e], masked[:, s, a:e],
                                         ACT.Copy).then_inc(dn_hi, 1)

            def shift_hi(v):
                ae.wait_ge(mod_placed, (4, 10)[v])
                nc.scalar.activation(sh_hi[:, v], sh[:, v], ACT.Copy).then_inc(sh_hi_ready, 1)

            def hi(number, k, h_hi, scale):
                ae.wait_ge(turned, number + k + 1)
                nc.scalar.activation(h_hi[:, k, :], bank[:, 2 + k % 2, :], ACT.Copy,
                                     scale=scale[:, k:k + 1]).then_inc(hi_ready, 1)

            def gelu(b, t):
                ae.wait_ge(y_done, b * 8 + t + 1)
                nc.scalar.activation(g[:, t, :], bank[:, t % 2, :], ACT.Gelu,
                                     bias=now_beta[:, t:t + 1]).then_inc(gelu_done, 1)

            def load_now1(b):
                if not at_start(b):
                    ae.wait_ge(lo_ready, turn1(b - 1) + FB)
                    ae.wait_ge(y_done, b * 8)
                nc.scalar.activation(now1[:], table[:, b, SCALE1:SCALE1 + FB], ACT.Copy).then_inc(now1_ready, 1)
                ae.wait_ge(now1_ready, b + 1)

            def iteration(b, has_y, has_prev, has_next):
                def load_ga():
                    nc.scalar.activation(now_ga[:], table[:, b, GA:GA + FB], ACT.Copy).then_inc(now_ga_ready, 1)

                if has_y:
                    if not has_prev:
                        ae.wait_ge(table_ready, 1)
                    else:
                        ae.wait_ge(back_done, b * 8)
                    nc.scalar.activation(now_beta[:], table[:, b, BETA1:BETA1 + FB],
                                         ACT.Copy).then_inc(now_beta_ready, 1)
                    if has_prev:
                        load_ga()
                    ae.wait_ge(now_beta_ready, b + 1)
                for t in range(FB):
                    if has_y:
                        gelu(b, t)
                    if has_y and not has_prev and t == 3:
                        ae.wait_ge(mod_placed, 6)
                        load_ga()
                    if has_prev and 3 <= t <= 6:
                        if t == 3:
                            ae.wait_ge(mod_placed, 8)
                            if not at_start(b - 1):
                                ae.wait_ge(pt_lo_ready, b * 2 - 2)
                            cols = FB if at_start(b - 1) else FB + RB
                            nc.scalar.activation(now2[:, 0:cols], table[:, b - 1, SCALE2:SCALE2 + cols],
                                                 ACT.Copy).then_inc(now2_ready, 1)
                            ae.wait_ge(now2_ready, b)
                        for k in (2 * (t - 3), 2 * (t - 3) + 1):
                            hi(turn2(b - 1), k, h2_hi, now2)
                    if at_start(b - 1, t == 4):
                        shift_hi(1)
                if has_next:
                    load_now1(b + 1)
                if has_y and not has_next:
                    for m in range(EARLY[0]):
                        weight_hi(m)
                elif not has_next:
                    for m in range(*EARLY):
                        weight_hi(m)
                for step in range(FB + T1_LAG):
                    if has_next and step >= T1_LAG:
                        hi(turn1(b + 1), step - T1_LAG, h1_hi, now1)
                    if has_prev and step == FB:
                        ae.wait_ge(p_done, b)
                        if at_start(b - 1):
                            ae.wait_ge(table_ready, 2)
                            nc.scalar.activation(now2[:, FB:FB + RB], table[:, 0, BETA2:BETA2 + RB],
                                                 ACT.Copy).then_inc(now_beta2_ready, 1)
                            ae.wait_ge(now_beta2_ready, 1)
                        else:
                            ae.wait_ge(pt_out, b * 16 - 16)
                        for r in range(RB):
                            nc.scalar.activation(pt_st[:, 0, r, :], bank[:, 6 + r, :], ACT.Identity,
                                                 bias=now2[:, FB + r:FB + r + 1]).then_inc(pt_hi_ready, 1)

            def weight_hi(m):
                if m == 0:
                    ae.wait_ge(y_done, FB * NB)
                    ae.wait_ge(mod_mm, NCHUNK)
                if m == piece_of["u2", 0] - 1:
                    ae.wait_ge(x2_out, 32 * NB)
                    ae.wait_ge(turned, 2 * FB * NB)
                    ae.wait_ge(back_done, FB * NB)
                if m == piece_of["u2", len(GROUPS) - 1] - 1:
                    ae.wait_ge(p_done, NB)
                if m == PIECES - NH:
                    ae.wait_ge(pt_out, 16 * NB)
                ae.wait_ge(raw_in[m % 3], raw_count[m])
                for part in pieces[m]:
                    nc.scalar.activation(part[5], raw_part(m % 3, part), ACT.Copy).then_inc(w_hi_ready, 1)

            EARLY = (2, 5)

            ae.wait_ge(mod_placed, 2)
            load_now1(0)
            for k in range(FB):
                hi(0, k, h1_hi, now1)
            shift_hi(0)
            iteration(0, True, False, True)
            iteration(1, True, True, True)
            with ae.Fori(2, NB - 1) as b:
                iteration(b, True, True, True)
            iteration(NB - 1, True, True, False)
            iteration(NB, False, True, False)

            def silu(b, q, i):
                w = width[i]
                ae.wait_ge(gate_done, b * IB + i + 1)
                if not at_start(b, i < 2):
                    ae.wait_ge(act_lo_ready, b * IB + i - 1)
                nc.scalar.activation(act[0:w, i % 2, :], bank[0:w, i % 2, :], ACT.Silu,
                                     bias=b1_sb[0:w, i, 0:1]).then_inc(silu_done, 1)

            def act_hi_part(b, q, i):
                w = width[i]
                slot = (q * IB + i) % 4
                ae.wait_ge(act_done, b * IB + i + 1)
                if not at_start(b, i < 4):
                    ae.wait_ge(z_step, b * IB + max(i - 3, 0))
                nc.scalar.activation(act_hi[0:w, slot, :], act[0:w, i % 2, :], ACT.Copy).then_inc(act_hi_ready, 1)

            def batch(b, q, last):
                for i in range(1, IB):
                    silu(b, q, i)
                    act_hi_part(b, q, i - 1)
                    if at_start(b, EARLY[1] + i - 1 < PIECES):
                        weight_hi(EARLY[1] + i - 1)
                act_hi_part(b, q, IB - 1)
                if not last:
                    silu(b + 1, 1 - q, 0)
                ae.wait_ge(z_step, b * IB + IB)
                if not at_start(b):
                    ae.wait_ge(o_mm, b * 8)
                for r in range(RB):
                    nc.scalar.activation(z_hi[:, r, :], bank[:, 4 + r, :], ACT.Copy).then_inc(z_hi_ready, 1)

            silu(0, 0, 0)
            batch(0, 0, False)
            with ae.Fori(1, NB // 2) as i:
                batch(i * 2 - 1, 1, False)
                batch(i * 2, 0, False)
            batch(NB - 1, 1, True)

        @block.vector
        def _(dve):
            steps = [0]

            def link(ins):
                steps[0] += 1
                ins.then_inc(dve_step, 1)
                dve.wait_ge(dve_step, steps[0])

            def stats1(b, halves):
                for m in halves:
                    src = x0 if at_start(b) else xs
                    if m == 0 and at_start(b):
                        dve.wait_ge(x0_in, 16)
                    elif m == 0:
                        dve.wait_ge(xs_in, b * 16)
                    n, h = m // NH, m % NH
                    nc.vector.bn_stats(bn1[:, n, h, :], src[:, n, h * HALF:(h + 1) * HALF]).then_inc(bn_done, 1)

            def aggregate(bn, mv, n, count, ready):
                if count is not None:
                    dve.wait_ge(bn_done, count)
                    nc.vector.memset(tick[:], 0.0)
                nc.vector.bn_aggr(mv[:, n, :], bn[:, n, :, :].rearrange("p h s -> p (h s)")).then_inc(ready, 1)

            def normalise(src, mv, rstd, ready, dst=nrm):
                for n in range(TT):
                    nc.vector.tensor_scalar(dst[:, n, :], src[:, n, :], mv[:, n, 0:1], rstd[:, n:n + 1],
                                            ALU.subtract, ALU.mult).then_inc(ready, 1)

            stats1(0, range(TT * NH))
            for n in range(TT):
                aggregate(bn1, mv1, n, 8 if n == 0 else None, mv1_ready)
            dve.wait_ge(rstd1_ready, 1)
            normalise(x0, mv1, rstd1, n1_ready, x0)

            for n, (s, a, e) in enumerate(off_band):
                dve.wait_ge(mask_in[2 * s // FB], 16)
                link(nc.vector.tensor_scalar(off_junk[:, 0:e - a], mask_sb[:, s, a:e], 0.0, 0.0, ALU.not_equal,
                                             ALU.max, accum_out=off_any[:, n:n + 1]))
            nc.vector.tensor_reduce(off_max[:], off_any[:], AX.X, ALU.max).then_inc(off_known, 1)

            def mask_product(src_bank, s, a, e, ready):
                nc.vector.tensor_tensor(masked[:, s, a:e], bank[:, src_bank, 0:e - a], mask_sb[:, s, a:e],
                                        ALU.mult).then_inc(ready, 1)

            def attn_rest(s, a, e, ready):
                nc.vector.tensor_tensor(attn_lo[:, s, a:e], masked[:, s, a:e], attn_hi[:, s, a:e],
                                        ALU.subtract).then_inc(ready, 1)

            for n, s in enumerate(BAND_ORDER):
                dve.wait_ge(attn_mm, n + 1)
                mask_product(s, s, *band_cols(s), masked_ready)
            for n, s in enumerate(BAND_ORDER):
                dve.wait_ge(attn_hi_ready, n + 1)
                attn_rest(s, *band_cols(s), attn_lo_ready)
            dve.wait_ge(flag_known, 1)
            dense = nc.vector.value_load(dense_flag[0:1, 0:1].bitcast(I32))
            with nc.vector.If(dense != 0):
                dve.wait_ge(attn_lo_ready, FB)
                for n, (s, a, e) in enumerate(off_band):
                    dve.wait_ge(dn_mm, n + 1)
                    mask_product(n % 2, s, a, e, dn_masked)
                    dve.wait_ge(dn_hi, n + 1)
                    attn_rest(s, a, e, dn_lo)

            def clamp_gate(dst):
                v = mod_sum[:]
                nc.vector.tensor_scalar(gate_sign[:], v, 0.0, 2.0, ALU.is_ge, ALU.mult)
                link(nc.vector.scalar_tensor_tensor(gate_size[:], v, -1.0, v, ALU.mult, ALU.max))
                link(nc.vector.tensor_scalar(gate_big[:], gate_size[:], GATE_FLOOR, None, ALU.max))
                return nc.vector.scalar_tensor_tensor(dst, gate_sign[:], -1.0, gate_big[:], ALU.add, ALU.mult)

            def mod_copy(q, rows_bank):
                dve.wait_ge(mod_mm, q + 1)
                if q >= 2:
                    dve.wait_ge(mod_turned, q - 1)
                nc.vector.tensor_copy(mod_rows[:, q % 2, :], bank[:, rows_bank, :]).then_inc(mod_rows_ready, 1)

            def mod_place(q, turn_bank):
                kind, j0 = KINDS[q // 2], q % 2 * 4
                dve.wait_ge(mod_turned, q + 1)
                if q >= 1:
                    dve.wait_ge(mod_placed, q)
                parts = bank[:, turn_bank, :].rearrange("p (k j c) -> p k c j", k=4, j=4)[:, :, 0:NB, :]
                nc.vector.tensor_reduce(mod_sum[:], parts, AX.X, ALU.add).then_inc(mod_read, 1)
                dve.wait_ge(mod_read, q + 1)
                if kind in (SA, SB):
                    last = nc.vector.tensor_copy(sh[:, kind // 3, j0:j0 + 4, :], mod_sum[:])
                elif kind in (CA, CB):
                    base = {CA: SCALE1, CB: SCALE2}[kind] + j0
                    last = nc.vector.tensor_scalar(table[:, :, base:base + 4].rearrange("p b j -> p j b"), mod_sum[:],
                                                   1.0, None, ALU.add)
                elif kind == GA_KIND:
                    last = clamp_gate(table[:, :, GA + j0:GA + j0 + 4].rearrange("p b j -> p j b"))
                else:
                    last = clamp_gate(gb_feat[:, j0:j0 + 4, :])
                last.then_inc(mod_placed, 1)

            def mod_pair(q):
                mod_copy(q, 6)
                mod_copy(q + 1, 7)
                mod_place(q, 4)
                mod_place(q + 1, 5)

            def shift_lo(v):
                dve.wait_ge(sh_hi_ready, v + 1)
                nc.vector.tensor_tensor(sh_lo[:, v], sh[:, v], sh_hi[:, v], ALU.subtract).then_inc(sh_lo_ready, 1)

            def beta2_rows():
                dve.wait_ge(beta_mm, 2)
                nc.vector.tensor_copy(beta_rows[:, 0, 0:R], bank[0:NB, 6, 0:R]).then_inc(beta_rows_ready, 1)

            def beta2_place():
                dve.wait_ge(beta_turned, 2)
                nc.vector.tensor_copy(table[:, :, BETA2:BETA2 + RB].rearrange("p b r -> p r b"),
                                      bank[:, 7, 0:RB * NB].rearrange("p (r b) -> p r b", r=RB))\
                    .then_inc(table_ready, 1)

            mod_pair(0)
            def lo(number, k, h_hi, h_lo, scale):
                dve.wait_ge(hi_ready, number + k + 1)
                nc.vector.scalar_tensor_tensor(h_lo[:, k, :], bank[:, 2 + k % 2, :], scale[:, k:k + 1],
                                               h_hi[:, k, :], ALU.mult, ALU.subtract).then_inc(lo_ready, 1)

            def iteration(b, has_y, has_prev, has_next):
                if at_start(b):
                    mod_pair(4)
                if has_prev:
                    dve.wait_ge(rstd2_ready, b)
                    dve.wait_ge(turned, turn2(NB - 1) if isinstance(b, int) and b == NB else turn1(b) + FB)
                    normalise(xr, mv2, rstd2, n2_ready)
                if has_y and not has_next:
                    dve.wait_ge(pt_out, b * 16 - 16)
                    mod_copy(10, 4)
                    mod_place(10, 5)
                if at_start(b - 1):
                    mod_copy(8, 6)
                    mod_copy(9, 7)
                for part, halves in enumerate(((0, 1, 2), (3, 4), (5, 6), (7,), ())):
                    if has_y and not has_next and part == 4:
                        mod_copy(11, 4)
                        mod_place(11, 5)
                    if has_next:
                        stats1(b + 1, halves)
                    if has_next and part == 3:
                        for n in range(TT):
                            aggregate(bn1, mv1, n, b * 16 + 16 if n == 0 else None, mv1_ready)
                    if has_prev and part < 4:
                        for k in (2 * part, 2 * part + 1):
                            lo(turn2(b - 1), k, h2_hi, h2_lo, now2)
                    if at_start(b - 1, part == 0):
                        mod_place(8, 4)
                        mod_place(9, 5)
                    elif at_start(b - 1, part == 1):
                        shift_lo(1)
                    elif at_start(b - 1, part == 2):
                        beta2_rows()
                    elif at_start(b - 1, part == 3):
                        beta2_place()
                if has_next:
                    dve.wait_ge(rstd1_ready, b + 2)
                    dve.wait_ge(turned, turn2(b - 1) + FB if has_prev else FB)
                    normalise(xs, mv1, rstd1, n1_ready)
                for step in range(FB + T1_LAG):
                    k = step - BACK_LAG
                    if has_y and 0 <= k < FB:
                        n, h = k // NH, k % NH
                        dve.wait_ge(back_done, b * 8 + k + 1)
                        if k % 4 == 0:
                            dve.wait_ge(xr_in[k // 4], b * 16 + 16)
                        half = xr[:, n, h * HALF:(h + 1) * HALF]
                        nc.vector.tensor_tensor(half, bank[:, 4 + h, :], half, ALU.add).then_inc(x2_ready, 1)
                    if has_next and step >= T1_LAG:
                        lo(turn1(b + 1), step - T1_LAG, h1_hi, h1_lo, now1)
                    if has_y and 0 <= k < FB:
                        dve.wait_ge(x2_ready, b * 8 + k + 1)
                        nc.vector.bn_stats(bn2[:, n, h, :], half).then_inc(bn_done, 1)
                        if h == 1:
                            after = b * 16 + 16 if has_next else b * 16 + 8
                            aggregate(bn2, mv2, n, after + k + 1, mv2_ready)
                    if has_prev and step == FB:
                        for r in range(RB):
                            dve.wait_ge(pt_hi_ready, b * 2 - 1 + r)
                            nc.vector.scalar_tensor_tensor(pt_st[:, 1, r, :], bank[:, 6 + r, :],
                                                           now2[:, FB + r:FB + r + 1], pt_st[:, 0, r, :],
                                                           ALU.add, ALU.subtract).then_inc(pt_lo_ready, 1)
                    if at_start(b, step == 4):
                        mod_copy(6, 6)
                    elif at_start(b, step == 6):
                        mod_copy(7, 7)
                        mod_place(6, 0)
                    elif at_start(b, step == 8):
                        mod_place(7, 1)

            for k in range(FB):
                lo(0, k, h1_hi, h1_lo, now1)
                if k == 3:
                    mod_copy(2, 6)
                elif k == 5:
                    mod_place(2, 4)
            mod_copy(3, 7)
            mod_place(3, 5)
            shift_lo(0)
            dve.wait_ge(beta_mm, 1)
            nc.vector.tensor_copy(beta_rows, bank[0:NB, 4:4 + NH, :]).then_inc(beta_rows_ready, 1)
            dve.wait_ge(beta_turned, 1)
            nc.vector.tensor_tensor(table[:, :, BETA1:BETA1 + FB].rearrange("p b t -> p t b"),
                                    bank[:, 2, 0:FB * NB].rearrange("p (t b) -> p t b", t=FB),
                                    b2_sb[:].unsqueeze(2).to_broadcast([P, FB, NB]), ALU.add).then_inc(table_ready, 1)
            iteration(0, True, False, True)
            iteration(1, True, True, True)
            with dve.Fori(2, NB - 1) as b:
                iteration(b, True, True, True)
            iteration(NB - 1, True, True, False)
            dve.wait_ge(gb_turned, 1)
            nc.vector.tensor_copy(gb_rows[:], bank[0:FB * NB, 4, 0:P]).then_inc(gb_ready, 1)
            iteration(NB, False, True, False)

            def multiply(b, q, i):
                w = width[i]
                if w == P:
                    up = bank[0:w, 2 + i % 2, :]
                    dve.wait_ge(up_done, b * (IB - 1) + i + 1)
                else:
                    up = bank[P - w:P, i % 2, :]
                    dve.wait_ge(gate_done, b * IB + i + 1)
                dve.wait_ge(silu_done, b * IB + i + 1)
                nc.vector.scalar_tensor_tensor(act[0:w, i % 2, :], up, b1_sb[0:w, i, 1:2],
                                               act[0:w, i % 2, :], ALU.add, ALU.mult).then_inc(act_done, 1)

            def act_lo_part(b, q, i):
                w = width[i]
                slot = (q * IB + i) % 4
                dve.wait_ge(act_hi_ready, b * IB + i + 1)
                nc.vector.tensor_tensor(act_lo[0:w, slot, :], act[0:w, i % 2, :], act_hi[0:w, slot, :],
                                        ALU.subtract).then_inc(act_lo_ready, 1)

            def batch(b, q, last):
                for i in range(2, IB):
                    multiply(b, q, i)
                    act_lo_part(b, q, i - 1)
                act_lo_part(b, q, IB - 1)
                for r in range(RB):
                    dve.wait_ge(z_hi_ready, b * 2 + r + 1)
                    nc.vector.tensor_tensor(z_lo[:, r, :], bank[:, 4 + r, :], z_hi[:, r, :],
                                            ALU.subtract).then_inc(z_lo_ready, 1)
                if not last:
                    multiply(b + 1, 1 - q, 0)
                if isinstance(b, int) and b == 0:
                    dve.wait_ge(b2f_in, 16)
                for m in range(TT * NH + 1):
                    if m < TT * NH:
                        dve.wait_ge(o_mm, b * 8 + m + 1)
                        if not at_start(b, m < 3):
                            dve.wait_ge(out_ready, b * 8 + (m - 2 if m >= 3 else (-1, 0, -2)[m]))
                        nc.vector.tensor_tensor(ffn[:, m % 3, :], bank[:, 6 + m % 2, :],
                                                b2f_bc[:, m % NH * HALF:(m % NH + 1) * HALF],
                                                ALU.add).then_inc(ffn_sum, 1)
                    if m == 1:
                        dve.wait_ge(gb_in, b * 16 + 16)
                    if m >= 1:
                        dve.wait_ge(ffn_sum, b * 8 + m)
                        slot, h = (m - 1) % 3, (m - 1) % NH
                        nc.vector.tensor_tensor(ffn[:, slot, :], ffn[:, slot, :], gb_bc[:, h * HALF:(h + 1) * HALF],
                                                ALU.mult).then_inc(ffn_ready, 1)
                    if m == 3 and not last:
                        multiply(b + 1, 1 - q, 1)
                    if m == 5 and not last:
                        act_lo_part(b + 1, 1 - q, 0)

            multiply(0, 0, 0)
            multiply(0, 0, 1)
            act_lo_part(0, 0, 0)
            batch(0, 0, False)
            with dve.Fori(1, NB // 2) as i:
                batch(i * 2 - 1, 1, False)
                batch(i * 2, 0, False)
            batch(NB - 1, 1, True)

        @block.gpsimd
        def _(pool):
            nc.gpsimd.memset(c_pad[:], 0.0).then_inc(zero_made, 1)
            nc.gpsimd.memset(ident[:], 0.0).then_inc(zero_made, 1)
            nc.gpsimd.memset(minus_half[:], -0.5).then_inc(zero_made, 1)
            nc.gpsimd.memset(eps[:], EPS).then_inc(zero_made, 1)
            pool.wait_ge(zero_made, 4)
            nc.gpsimd.affine_select(out=ident[:], in_=ident[:], compare_op=ALU.not_equal, fill=1.0, base=0,
                                    pattern=[[-1, P]], channel_multiplier=1).then_inc(consts_made, 1)
            def rstd(mv, ve, dst, mv_ready, count, ve_count, ready):
                pool.wait_ge(mv_ready, count)
                nc.gpsimd.tensor_tensor(ve[:], mv[:, :, 1], eps[:], ALU.add).then_inc(ve_ready, 1)
                pool.wait_ge(ve_ready, ve_count)
                nc.gpsimd.tensor_tensor(dst[:], ve[:], minus_half[:], ALU.pow).then_inc(ready, 1)

            def gate(b, t):
                if t == 0:
                    pool.wait_ge(now_ga_ready, b + 1)
                pool.wait_ge(gelu_done, b * 8 + t + 1)
                nc.gpsimd.tensor_tensor(g[:, t, :], g[:, t, :], now_ga[:, t:t + 1].to_broadcast([P, TOK]),
                                        ALU.mult).then_inc(g_ready, 1)

            rstd(mv1, ve1, rstd1, mv1_ready, 4, 1, rstd1_ready)
            pool.wait_ge(off_known, 1)
            nc.gpsimd.partition_all_reduce(dense_flag[:], off_max[:], P, bass.bass_isa.ReduceOp.max)\
                .then_inc(flag_known, 1)
            pool.wait_ge(u1_in, 16)
            pool.wait_ge(attn_lo_ready, FB)
            pool.wait_ge(turned, FB)
            u1_raw = xr[:, 0:2, :].rearrange("p n d -> p (n d)").rearrange("p (k r) -> p k r", k=FB)
            nc.gpsimd.tensor_copy(u1_hi[:], u1_raw).then_inc(u1_hi_ready, 1)
            pool.wait_ge(u1_hi_ready, 1)
            nc.gpsimd.tensor_tensor(u1_lo[:], u1_raw, u1_hi[:], ALU.subtract).then_inc(u1_ready, 1)

            def weight_lo(m):
                for n, part in enumerate(pieces[m]):
                    pool.wait_ge(w_hi_ready, sum(len(p) for p in pieces[:m]) + n + 1)
                    last = nc.gpsimd.tensor_tensor(part[6], raw_part(m % 3, part), part[5], ALU.subtract)
                last.then_inc(w_ready, 1)

            def iteration(b, has_next):
                before = 3 if at_start(b) else 6
                for t in range(before):
                    gate(b, t)
                if has_next:
                    rstd(mv1, ve1, rstd1, mv1_ready, b * 4 + 8, b * 2 + 2, rstd1_ready)
                for t in range(before, FB):
                    gate(b, t)
                if not has_next:
                    weight_lo(0)
                rstd(mv2, ve2, rstd2, mv2_ready, b * 4 + 4, b * 2 + 3 if has_next else b * 2 + 2, rstd2_ready)

            iteration(0, True)
            with pool.Fori(1, NB - 1) as b:
                iteration(b, True)
            iteration(NB - 1, False)

            for m in range(1, PIECES):
                weight_lo(m)

            def residual(b):
                for m in range(TT * NH):
                    n, h = m // NH, m % NH
                    half = x2t[:, n, h * HALF:(h + 1) * HALF]
                    if h == 0:
                        pool.wait_ge(x2t_in[n], b * 16 + 16)
                    pool.wait_ge(ffn_ready, b * 8 + m + 1)
                    nc.gpsimd.tensor_tensor(half, ffn[:, m % 3, :], half, ALU.add).then_inc(out_ready, 1)

            with pool.Fori(0, NB) as b:
                residual(b)


_NAMES = ["x", "w1", "w2t", "b2", "mask", "u1", "v1", "u2", "v2", "b1_main", "b1_tail", "b2f", "ct", "wmod"]


def kernel(**inputs):
    import numpy as np
    import concourse.bacc as bacc
    from concourse.bass_utils import run_bass_kernel_spmd as run

    def get(name):
        return np.asarray(inputs["L0_" + name])

    b1 = get("ffn_b1").reshape(2, -1)
    inter = b1.shape[1]
    whole = inter // P * P
    assert whole < inter
    laid = {
        "x": get("attn_x"),
        "w1": get("attn_w1"),
        "w2t": get("attn_w2").T,
        "b2": get("attn_b2").reshape(-1, P).T,
        "mask": get("attn_sparse_mask"),
        "u1": get("ffn_U1"),
        "v1": get("ffn_V1"),
        "u2": get("ffn_U2"),
        "v2": get("ffn_V2"),
        "b1_main": b1[:, :whole].reshape(2, -1, P).transpose(2, 1, 0),
        "b1_tail": b1[:, whole:].T.reshape(inter - whole, 1, 2),
        "b2f": get("ffn_b2").reshape(1, -1),
        "ct": get("c").T,
        "wmod": get("wmod"),
    }
    nc = bacc.Bacc("TRN2", target_bir_lowering=False, num_devices=1, dynamic_dma_scratch_size=1024)
    arrays, args = {}, []
    for name in _NAMES:
        a = np.ascontiguousarray(laid[name])
        arrays[f"in_{name}"] = a
        args.append(nc.dram_tensor(f"in_{name}", a.shape, mybir.dt.from_np(a.dtype), kind="ExternalInput").ap())
    out = nc.dram_tensor("out", laid["x"].shape, F32, kind="ExternalOutput").ap()
    adaln_block(nc, *args, out)
    result = run(nc, [arrays], core_ids=[0])
    return result.results[0]["out"]
```
